# Optimizing a Trainium2 kernel written in Bass

```python
import numpy as np
import jax
import jax.numpy as jnp

def _softmax(x, axis=-1):
    return jax.nn.softmax(x, axis=axis)

def _gelu(x):
    return jax.nn.gelu(x, approximate=True)

def _silu(x):
    return jax.nn.silu(x)

def _sigmoid(x):
    return jax.nn.sigmoid(x)

def _layernorm(x, axis=-1, eps=1e-05):
    m = jnp.mean(x, axis=axis, keepdims=True)
    v = jnp.var(x, axis=axis, keepdims=True)
    return (x - m) / jnp.sqrt(v + eps)

def _scatter_add(tgt, idx, src, axis=0):
    return tgt.at[idx].add(src)

def _segment_sum(src, seg, n):
    return jax.ops.segment_sum(src, seg, n)
kernel_name = 'mk_gnn_resnorm_d2_gnn_r16_6e7d3a'

def setup_inputs(seed: int=0):
    np.random.seed(seed)
    _w = jnp.asarray

    def _rec_inputs():
        import jax
        import jax.numpy as jnp
        _gk = jax.random.key(seed)
        x = -0.0006008 + 1.001 * jax.random.normal(jax.random.fold_in(_gk, 1), (6250, 256), jnp.float32)
        src = jax.random.randint(jax.random.fold_in(_gk, 2), (100000,), 0, 6250, jnp.int32)
        dst = jnp.minimum((6250 * jax.random.uniform(jax.random.fold_in(_gk, 3), (100000,)) ** 2.0).astype(jnp.int32), 99999)
        _o = jnp.argsort(dst, stable=True)
        src = src[_o]
        dst = dst[_o]
        edge_attr_64 = -9.77346e-05 + 0.999888 * jax.random.normal(jax.random.fold_in(_gk, 12), (100000, 64), jnp.float32)
        return (x, src, dst, edge_attr_64)
    x, src, dst, edge_attr_64 = _rec_inputs()

    def _L0_gnn_setup():
        import jax, jax.numpy as jnp
        import numpy as np
        N_NODES = 625
        N_EDGES = 20000
        D = 256
        key = jax.random.key(seed)
        k1, k2, k3, k4, k5 = jax.random.split(key, 5)
        x = jax.random.normal(k1, (N_NODES, D), dtype=jnp.float32)
        src = jax.random.randint(k2, (N_EDGES,), 0, N_NODES, dtype=jnp.int32)
        dst = jax.random.randint(k3, (N_EDGES,), 0, N_NODES, dtype=jnp.int32)
        s = 1.0 / np.sqrt(D)
        theta_w = jax.random.uniform(k4, (D, D), jnp.float32, -s, s)
        theta_b = jnp.zeros((D,), jnp.float32)
        phi_w = jax.random.uniform(k5, (D, D), jnp.float32, -s, s)
        phi_b = jnp.zeros((D,), jnp.float32)
        return {'x': x, 'src': src, 'dst': dst, 'theta_w': theta_w, 'theta_b': theta_b, 'phi_w': phi_w, 'phi_b': phi_b}
    _L0_gnn_all = _L0_gnn_setup()
    _L0_gnn_in = {k: v for k, v in _L0_gnn_all.items() if k in ('theta_w', 'theta_b', 'phi_w', 'phi_b')}
    del _L0_gnn_all

    def _L1_gnn_setup():
        import jax, jax.numpy as jnp
        import numpy as np
        N_NODES = 3125
        N_EDGES = 50000
        FEAT = 256
        EDIM = 64
        OUT = 256
        key = jax.random.key(seed)
        ks = jax.random.split(key, 12)
        s_in = 1.0 / np.sqrt(FEAT)
        s_u = 1.0 / np.sqrt(OUT + EDIM)
        s_ro = 1.0 / np.sqrt(OUT)
        return {'x': jax.random.normal(ks[0], (N_NODES, FEAT), jnp.float32), 'he': jax.random.normal(ks[1], (N_EDGES, EDIM), jnp.float32), 'src': jax.random.randint(ks[2], (N_EDGES,), 0, N_NODES, jnp.int32), 'dst': jax.random.randint(ks[3], (N_EDGES,), 0, N_NODES, jnp.int32), 'W_in': jax.random.normal(ks[4], (FEAT, OUT), jnp.float32) * s_in, 'b_in': jnp.zeros((OUT,), jnp.float32), 'W_u0': jax.random.normal(ks[5], (OUT + EDIM, OUT), jnp.float32) * s_u, 'b_u0': jnp.zeros((OUT,), jnp.float32), 'W_u1': jax.random.normal(ks[6], (OUT + EDIM, OUT), jnp.float32) * s_u, 'b_u1': jnp.zeros((OUT,), jnp.float32), 'W_ro': jax.random.normal(ks[7], (OUT, OUT), jnp.float32) * s_ro, 'b_ro': jnp.zeros((OUT,), jnp.float32)}
    _L1_gnn_all = _L1_gnn_setup()
    _L1_gnn_in = {k: v for k, v in _L1_gnn_all.items() if k in ('W_in', 'b_in', 'W_u0', 'b_u0', 'W_u1', 'b_u1', 'W_ro', 'b_ro')}
    del _L1_gnn_all
    return {'x': x, 'src': src, 'dst': dst, 'edge_attr_64': edge_attr_64, 'L0_gnn_theta_w': _L0_gnn_in['theta_w'], 'L0_gnn_theta_b': _L0_gnn_in['theta_b'], 'L0_gnn_phi_w': _L0_gnn_in['phi_w'], 'L0_gnn_phi_b': _L0_gnn_in['phi_b'], 'L1_gnn_W_in': _L1_gnn_in['W_in'], 'L1_gnn_b_in': _L1_gnn_in['b_in'], 'L1_gnn_W_u0': _L1_gnn_in['W_u0'], 'L1_gnn_b_u0': _L1_gnn_in['b_u0'], 'L1_gnn_W_u1': _L1_gnn_in['W_u1'], 'L1_gnn_b_u1': _L1_gnn_in['b_u1'], 'L1_gnn_W_ro': _L1_gnn_in['W_ro'], 'L1_gnn_b_ro': _L1_gnn_in['b_ro']}

def reference(x, src, dst, edge_attr_64, L0_gnn_theta_w, L0_gnn_theta_b, L0_gnn_phi_w, L0_gnn_phi_b, L1_gnn_W_in, L1_gnn_b_in, L1_gnn_W_u0, L1_gnn_b_u0, L1_gnn_W_u1, L1_gnn_b_u1, L1_gnn_W_ro, L1_gnn_b_ro):
    import jax
    import jax.numpy as jnp

    def _L0_gnn_ref(x, src, dst, theta_w, theta_b, phi_w, phi_b):
        import jax, jax.numpy as jnp
        import numpy as np
        N_NODES = 625
        N_EDGES = 20000
        D = 256
        x_src = x[src]
        x_dst = x[dst]
        theta_x = (x_dst - x_src) @ theta_w.T + theta_b
        phi_x = x_src @ phi_w.T + phi_b
        e = jax.nn.relu(theta_x + phi_x)
        out = jax.ops.segment_max(e, dst, num_segments=x.shape[0])
        return jnp.where(jnp.isfinite(out), out, 0.0)

    def _L1_gnn_ref(x, he, src, dst, W_in, b_in, W_u0, b_u0, W_u1, b_u1, W_ro, b_ro):
        import jax, jax.numpy as jnp
        import numpy as np
        N_NODES = 3125
        N_EDGES = 50000
        FEAT = 256
        EDIM = 64
        OUT = 256
        n = x.shape[0]
        hv = x @ W_in + b_in
        deg = jax.ops.segment_sum(jnp.ones_like(dst, jnp.float32), dst, num_segments=n)
        has_in = (deg > 0)[:, None]
        for W, b in ((W_u0, b_u0), (W_u1, b_u1)):
            m = jnp.concatenate([hv[src], he], axis=-1)
            m = jax.nn.relu(m @ W + b)
            msg = jax.ops.segment_max(m, dst, num_segments=n)
            hv = jnp.where(has_in, msg + hv, hv)
        return jax.nn.relu(hv @ W_ro + b_ro)
    x = _layernorm(x + _L0_gnn_ref(x, src, dst, L0_gnn_theta_w, L0_gnn_theta_b, L0_gnn_phi_w, L0_gnn_phi_b), axis=-1)
    x = _layernorm(x + _L1_gnn_ref(x, edge_attr_64, src, dst, L1_gnn_W_in, L1_gnn_b_in, L1_gnn_W_u0, L1_gnn_b_u0, L1_gnn_W_u1, L1_gnn_b_u1, L1_gnn_W_ro, L1_gnn_b_ro), axis=-1)
    return x

_drawn_inputs = setup_inputs


def setup_inputs(seed=0):
    import zlib

    import numpy as np

    out = dict(_drawn_inputs(seed))
    spreads = {'L0_gnn_theta_b': (0.0, 0.1),
     'L0_gnn_phi_b': (0.0, 0.1),
     'L1_gnn_b_in': (0.0, 0.1),
     'L1_gnn_b_u0': (0.0, 0.1),
     'L1_gnn_b_u1': (0.0, 0.338),
     'L1_gnn_b_ro': (0.0, 0.315)}
    factors = {}
    for name, (base, spread) in spreads.items():
        noise = np.random.default_rng([zlib.crc32(name.encode()), seed]).standard_normal(out[name].shape)
        drawn = base * np.exp(spread * noise) if base else spread * noise
        out[name] = jnp.asarray(drawn.astype(out[name].dtype))
    for name, factor in factors.items():
        out[name] = (out[name] * factor).astype(out[name].dtype)
    return out
```

```python
import concourse.bass as bass
from concourse import mybir
from concourse.alu_op_type import AluOpType as ALU
from contextlib import ExitStack

P = 128
NODES, EDGES, D, ED = 6250, 100000, 256, 64
KH = D // P
BODY = 16
TURNS = -(-EDGES // (P * BODY))
STEPS = TURNS * BODY
SLOTS = P * STEPS
CH = 4
NCH = BODY // CH
PAIRS = BODY // 2
BANKS = 4
HALF = BODY // 2
TILES = -(-NODES // P)
GT = 7
GROUPS = TILES // GT
NPAD = TILES * P
ROUNDS = 3
EPS = 1e-5
LOWEST = -3.0e38
FAR = 1 << 20
QSTEPS = 9
assert GROUPS * GT == TILES and TURNS == TILES


def gnn_kernel(nc, a):
    f32, bf16, i32 = mybir.dt.float32, mybir.dt.bfloat16, mybir.dt.int32
    ACT = mybir.ActivationFunctionType

    tables = [nc.dram_tensor(f"table{r}", [NPAD, D], f32, kind="Internal").ap() for r in range(ROUNDS)]
    runs = nc.dram_tensor("runs", [SLOTS + P, D], f32, kind="Internal").ap()
    runs_by_part = runs[0:SLOTS, :].rearrange("(p t) f -> p t f", p=P)
    halves = lambda w: w.rearrange("(h k) o -> k h o", h=KH)

    ctx = ExitStack()
    with ctx:
        def sb(name, shape, dt=f32):
            return ctx.enter_context(nc.sbuf_tensor(name, shape, dt))

        def sem(name):
            return ctx.enter_context(nc.semaphore(name))

        x_sb = sb("x_sb", [P, TILES, D])
        hv_sb = sb("hv_sb", [P, TILES, D])
        gath = sb("gath", [P, BODY, D])
        hist = sb("hist", [P, BODY, D])
        he_sb = sb("he_sb", [P, NCH, CH // 2 * P])
        src_sb = sb("src_sb", [P, STEPS], i32)
        dst_i = sb("dst_i", [P, STEPS], i32)
        dst_f = sb("dst_f", [P, STEPS + 1])
        keep = sb("keep", [P, STEPS])
        lift = sb("lift", [P, STEPS])
        idx_ring = sb("idx_ring", [P, BODY], i32)
        end_idx = sb("end_idx", [P, TILES + GT], i32)
        end_ring = sb("end_ring", [P, GT], i32)
        has = sb("has", [P, TILES])
        fix_from = sb("fix_from", [P, 1], i32)
        fix_to = sb("fix_to", [P, 1], i32)
        fix_rows = sb("fix_rows", [P, D])
        fix_T = sb("fix_T", [P, KH, P])
        lastrow = sb("lastrow", [P, P])
        lastrow_i = sb("lastrow_i", [P, P], i32)
        joins = sb("joins", [P, P])
        joins_lift = sb("joins_lift", [P, P])
        w_conv = sb("w_conv", [P, KH, 2 * D])
        w_phi = sb("w_phi", [P, KH, D])
        w_in = sb("w_in", [P, KH, 2 * D])
        w_inT = sb("w_inT", [P, KH, D])
        w_n0 = sb("w_n0", [P, KH, D])
        w_n1 = sb("w_n1", [P, KH, D])
        w_ro = sb("w_ro", [P, KH, D])
        w_e = [sb(f"w_e{r}", [P, 2 * D]) for r in range(2)]
        b_in_col = sb("b_in_col", [P, KH])
        b_in_cols = sb("b_in_cols", [P, KH, P])
        b_full = [sb(f"b_full{n}", [P, 2 * D]) for n in range(4)]
        b_add = sb("b_add", [P, 2 * D])
        b_parts = [sb(f"b_parts{n}", [P, 2 * D], bf16) for n in range(4)]
        rest = sb("rest", [P, 2 * D])
        part = [sb(f"part{n}", [P, 2 * D], bf16) for n in range(3)]
        row_is = sb("row_is", [P, 3])
        ones_bf = sb("ones_bf", [P, P], bf16)
        ident = sb("ident", [P, P])
        col_no = sb("col_no", [P, P])
        part_no = sb("part_no", [P, 1])
        node_no = sb("node_no", [P, 1])
        bounds = sb("bounds", [P, 2])
        bounds_fix = sb("bounds_fix", [P, 2])
        next_i = sb("next_i", [P, 2], i32)
        next_f = sb("next_f", [P, 2])
        first_f = sb("first_f", [P, 1])
        onehot = sb("onehot", [P, P])
        above = sb("above", [P, P])
        junk = sb("junk", [P, STEPS])
        counts = sb("counts", [P, 3])
        at_end = sb("at_end", [P, 4])
        stats = sb("stats", [P, GT, nc.vector.BN_STATS_DIM])
        mv = sb("mv", [P, GT, nc.vector.BN_AGGR_DIM])
        std = sb("std", [P, GT])
        rstd = sb("rstd", [P, GT])
        eps_col = sb("eps_col", [P, 1])

        rows_in = [gath[:, k, :] for k in range(GT)]
        work = [gath[:, GT + k, :] for k in range(GT)]
        xT_ring = rows_in
        turned = [hist[:, k, :] for k in range(GT)]
        staged = [hist[:, GT + k, :] for k in range(GT)]

        edge_ps = ctx.enter_context(nc.psum_tensor("edge_ps", [P, BANKS, 2 * D], f32))
        node_ps = ctx.enter_context(nc.psum_tensor("node_ps", [P, 2, 2 * D], f32))
        turn_ps = ctx.enter_context(nc.psum_tensor("turn_ps", [P, 2, 2 * D], f32))
        query_ps = node_ps[:, :, :].rearrange("p b f -> p (b f)")

        w_loaded = sem("w_loaded")
        x_loaded = sem("x_loaded")
        consts_made = sem("consts_made")
        setup_step = sem("setup_step")
        setup_mm = sem("setup_mm")
        xT_landed = [sem(f"xT_landed{k}") for k in range(GT)]
        staged_written = [sem(f"staged_written{k}") for k in range(GT)]
        waits_met = sem("waits_met")
        idx_ready = sem("idx_ready")
        gathered = [sem(f"gathered{c}") for c in range(NCH)]
        he_loaded = [sem(f"he_loaded{c}") for c in range(NCH)]
        pair_summed = sem("pair_summed")
        state_done = sem("state_done")
        stored = [sem(f"stored{h}") for h in range(2)]
        query = sem("query")
        dst_rows = sem("dst_rows")
        fix_turned = sem("fix_turned")
        fix_scanned = sem("fix_scanned")
        fix_back = sem("fix_back")
        fix_read = sem("fix_read")
        fix_joined = sem("fix_joined")
        fix_written = sem("fix_written")
        end_ready = sem("end_ready")
        row_landed = [sem(f"row_landed{k}") for k in range(GT)]
        row_used = sem("row_used")
        relu_done = sem("relu_done")
        norm_step = sem("norm_step")
        std_ready = sem("std_ready")
        tile_ready = sem("tile_ready")
        turned_ps = sem("turned_ps")
        turned_out = sem("turned_out")
        product = sem("product")
        product_out = sem("product_out")
        hv_kept = sem("hv_kept")
        out_ready = sem("out_ready")

        weight_loads = [
            (w_conv[:, :, D:], halves(a["theta_wT"])), (w_phi[:, :, :], halves(a["phi_wT"])),
            (b_full[0][:, D:], a["theta_b"].partition_broadcast(P)),
            (b_add[:, D:], a["phi_b"].partition_broadcast(P)),
            (dst_i[:, :], a["dst"]), (src_sb[:, :], a["src"]),
            (next_i[0:P - 1, 0:1], a["dst"][1:P, 0:1]), (next_i[0:P - 1, 1:2], a["dst"][1:P, STEPS - 1:STEPS]),
            (lastrow_i[:, :], a["dst_last"].partition_broadcast(P)),
            (w_in[:, :, 0:D], halves(a["W_in"])), (w_inT[:, :, :], halves(a["W_inT"])),
            (w_n0[:, :, :], halves(a["W_u0"][0:D, :])), (w_n1[:, :, :], halves(a["W_u1"][0:D, :])),
            (w_ro[:, :, :], halves(a["W_ro"])),
            (b_in_col[:, :], a["b_in"].rearrange("(h k) -> k h", h=KH)),
            (b_full[1][:, 0:D], a["b_in"].partition_broadcast(P)),
            (b_add[:, 0:D], a["b_u0"].partition_broadcast(P)),
            (b_full[2][:, 0:D], a["b_u1"].partition_broadcast(P)),
            (b_full[3][:, 0:D], a["b_ro"].partition_broadcast(P)),
        ] + [(w_e[r][ED * s:ED * (s + 1), D * s:D * (s + 1)], a[f"W_u{r}"][D:D + ED, :])
             for r in range(2) for s in range(2)]
        W_ALL = 16 * len(weight_loads)
        CLEARS = 3 + 4

        CONV_READY, BIAS0_READY, QUERY_READY, IN_COLS_READY, WIN_STEP, SETUP_ALL = range(6)
        setup_at = {}

        block = ctx.enter_context(nc.Block())

        NORM = 4

        @block.vector
        def _(dve):
            done = [0]
            V = nc.vector

            def after():
                if done[0]:
                    dve.wait_ge(setup_step, done[0])

            def step(ins):
                ins.then_inc(setup_step, 1)
                done[0] += 1

            dve.sem_inc(state_done, 2 * BANKS)
            dve.sem_inc(row_used, GT)
            step(V.memset(next_i[:, :], FAR))
            step(V.memset(w_e[0][:, :], 0.0))
            step(V.memset(w_e[1][:, :], 0.0))
            for n in range(4):
                step(V.memset(b_full[n][:, :], 0.0))
            assert done[0] == CLEARS
            step(V.memset(hist[:, BODY - 1, :], 0.0))
            step(V.memset(end_idx[:, :], 0))
            step(V.memset(ones_bf[:, :], 1.0))
            step(V.memset(eps_col[:, :], EPS))
            dve.wait_ge(consts_made, 2)
            step(V.tensor_scalar(ident[:, :], col_no[:, :], part_no[:, 0:1], None, ALU.is_equal))
            for n in range(3):
                step(V.tensor_scalar(row_is[:, n:n + 1], part_no[:, :], float(n), None, ALU.is_equal))
            dve.wait_ge(w_loaded, W_ALL)
            step(V.tensor_tensor(w_conv[:, :, 0:D], w_phi[:, :, :], w_conv[:, :, D:], ALU.subtract))
            step(V.tensor_tensor(b_full[0][:, D:], b_full[0][:, D:], b_add[:, D:], ALU.add))

            def split_bias(n):
                after()
                step(V.tensor_copy(part[0][:, :], b_full[n][:, :]))
                after()
                step(V.tensor_tensor(rest[:, :], b_full[n][:, :], part[0][:, :], ALU.subtract))
                after()
                step(V.tensor_copy(part[1][:, :], rest[:, :]))
                after()
                step(V.tensor_tensor(rest[:, :], rest[:, :], part[1][:, :], ALU.subtract))
                after()
                step(V.tensor_copy(part[2][:, :], rest[:, :]))
                step(V.tensor_scalar(b_parts[n][:, :], part[0][:, :], row_is[:, 0:1], None, ALU.mult))
                for m in (1, 2):
                    after()
                    step(V.scalar_tensor_tensor(b_parts[n][:, :], part[m][:, :], row_is[:, m:m + 1], b_parts[n][:, :],
                                                ALU.mult, ALU.add))

            split_bias(0)
            setup_at[BIAS0_READY] = done[0]
            for h in range(KH):
                step(V.tensor_copy(b_in_cols[:, h, :], b_in_col[:, h:h + 1].to_broadcast([P, P])))
            setup_at[IN_COLS_READY] = done[0]

            step(V.tensor_copy(dst_f[:, 0:STEPS], dst_i[:, :]))
            step(V.tensor_scalar(dst_f[:, STEPS:], part_no[:, :], float(STEPS), None, ALU.mult))
            step(V.tensor_copy(next_f[:, :], next_i[:, :]))
            step(V.tensor_copy(lastrow[:, :], lastrow_i[:, :]))
            step(V.memset(keep[:, 0:1], 0.0))
            step(V.memset(joins[:, 0:1], 0.0))
            after()
            step(V.tensor_tensor(keep[:, 1:], dst_f[:, 1:STEPS], dst_f[:, 0:STEPS - 1], ALU.is_equal))
            step(V.tensor_tensor(joins[:, 1:], lastrow[:, 1:], lastrow[:, 0:P - 1], ALU.is_equal))
            step(V.tensor_copy(bounds[:, 0:1], dst_f[:, 0:1]))
            step(V.tensor_copy(bounds[:, 1:2], next_f[:, 0:1]))
            after()
            step(V.memset(bounds[0:1, 0:1], 0.0))
            step(V.tensor_scalar(lift[:, :], keep[:, :], 1.0, -LOWEST, ALU.subtract, ALU.mult))
            step(V.tensor_scalar(joins_lift[:, :], joins[:, :], 1.0, -LOWEST, ALU.subtract, ALU.mult))
            step(V.tensor_copy(node_no[:, :], part_no[:, :]))
            after()
            setup_at[QUERY_READY] = done[0]

            def pick_rows(q, along):
                dve.wait_ge(query, QSTEPS * q + 1)
                V.tensor_scalar(above[:, :], along, bounds[:, 0:1], None, ALU.is_ge).then_inc(query, 1)
                dve.wait_ge(query, QSTEPS * q + 2)
                V.scalar_tensor_tensor(onehot[:, :], along, bounds[:, 1:2], above[:, :], ALU.is_lt,
                                       ALU.mult).then_inc(query, 1)

            def find_ends(q, nodes, at, has_at, shift):
                dve.wait_ge(dst_rows, q + 1)
                V.tensor_scalar(junk[:, :], query_ps[:, 0:STEPS], nodes, 0.0, ALU.is_le, ALU.add,
                                accum_out=counts[:, 0:1]).then_inc(query, 1)
                dve.wait_ge(query, QSTEPS * q + 4)
                V.tensor_scalar(junk[:, :], query_ps[:, 0:STEPS], nodes, 0.0, ALU.is_lt, ALU.add,
                                accum_out=counts[:, 1:2]).then_inc(query, 1)
                V.tensor_scalar(counts[:, 2:3], counts[:, 0:1], query_ps[:, STEPS:STEPS + 1], -1.0, ALU.add,
                                ALU.add).then_inc(query, 1)
                dve.wait_ge(query, QSTEPS * q + 6)
                V.tensor_scalar(at, counts[:, 2:3], 0.0, None, ALU.max).then_inc(query, 1)
                V.tensor_tensor(has_at, counts[:, 0:1], counts[:, 1:2], ALU.is_gt).then_inc(query, 1)
                V.tensor_scalar(bounds[:, :], bounds[:, :], shift, None, ALU.subtract).then_inc(query, 1)
                V.tensor_scalar(node_no[:, :], node_no[:, :], shift, None, ALU.add).then_inc(query, 1)

            dve.sem_inc(query, 1)
            pick_rows(0, lastrow[:, :])
            find_ends(0, dst_f[:, STEPS - 1:STEPS], at_end[:, 0:1], at_end[:, 1:2], 0.0)
            dve.wait_ge(query, QSTEPS + 1)
            step(V.tensor_copy(fix_from[:, :], at_end[:, 0:1]))
            step(V.tensor_tensor(at_end[:, 2:3], dst_f[:, STEPS - 1:STEPS], next_f[:, 1:2], ALU.not_equal))
            step(V.tensor_scalar(at_end[:, 3:4], part_no[:, :], float(SLOTS), None, ALU.add))
            after()
            step(V.tensor_tensor(at_end[:, 0:1], at_end[:, 0:1], at_end[:, 3:4], ALU.subtract))
            after()
            step(V.scalar_tensor_tensor(fix_to[:, :], at_end[:, 0:1], at_end[:, 2:3], at_end[:, 3:4], ALU.mult, ALU.add))

            dve.wait_ge(setup_mm, 1)
            step(V.tensor_copy(w_in[:, :, D:], turn_ps[:, :, 0:D]))
            step(V.tensor_tensor(b_full[1][:, D:], turn_ps[:, 0, D:], b_add[:, 0:D], ALU.add))
            for n in range(1, 4):
                split_bias(n)
            setup_at[SETUP_ALL] = done[0]

            def edge_maxima(r, i):
                for j in range(BODY):
                    if r == 0 and j == HALF:
                        pick_rows(i + 1, col_no[:, :])
                    if j % HALF == 0:
                        dve.wait_ge(stored[j // HALF], (r * TURNS + i + 1) * 16)
                    if j % 2 == 0:
                        dve.wait_ge(pair_summed, (r * TURNS + i) * PAIRS + j // 2 + 1 + PAIRS)
                    dve.wait_ge(state_done, (r * TURNS + i) * BODY + j + 2 * BANKS)
                    fresh = lift if r == 0 else keep
                    V.scalar_tensor_tensor(hist[:, j, :], hist[:, (j - 1) % BODY, :], fresh[:, bass.ds(i * BODY + j, 1)],
                                           edge_ps[:, (j // 2) % BANKS, (j % 2) * D:(j % 2 + 1) * D],
                                           ALU.add if r == 0 else ALU.mult, ALU.max).then_inc(state_done, 1)
                if r == 0:
                    find_ends(i + 1, node_no[:, 0:1], end_idx[:, bass.ds(i, 1)], has[:, bass.ds(i, 1)], float(P))

            def join_runs(r):
                dve.wait_ge(fix_turned, r + 1)
                for h in range(KH):
                    V.tensor_tensor_scan(fix_T[:, h, :], (joins_lift if r == 0 else joins)[:, :],
                                         turn_ps[:, 0, h * P:(h + 1) * P], 0.0,
                                         ALU.add if r == 0 else ALU.mult, ALU.max).then_inc(fix_scanned, 1)
                dve.wait_ge(fix_back, r + 1)
                dve.wait_ge(fix_read, 16 * (r + 1))
                V.tensor_tensor(fix_rows[:, :], turn_ps[:, 1, 0:D], fix_rows[:, :], ALU.max).then_inc(fix_joined, 1)

            def normalise(n, g, tiles, add, ready):
                base = NORM * ((n * GROUPS + g) * GT)
                for k in range(GT):
                    if n == 0:
                        dve.wait_ge(relu_done, g * GT + k + 1)
                    else:
                        dve.wait_ge(product_out, ROUNDS * TILES + g * GT + k + 1 + 2)
                    V.tensor_tensor(tiles[k], tiles[k], add(k), ALU.add).then_inc(norm_step, 1)
                    dve.wait_ge(norm_step, base + 2 * k + 1)
                    V.bn_stats(stats[:, k, :], tiles[k]).then_inc(norm_step, 1)
                dve.wait_ge(norm_step, base + 2 * GT)
                dve.sem_inc(waits_met, 1)
                for k in range(GT):
                    V.bn_aggr(mv[:, k, :], stats[:, k, :]).then_inc(norm_step, 1)
                for k in range(GT):
                    dve.wait_ge(std_ready, (n * GROUPS + g) * GT + k + 1)
                    V.reciprocal(rstd[:, k:k + 1], std[:, k:k + 1]).then_inc(norm_step, 1)
                for k in range(GT):
                    dve.wait_ge(norm_step, base + 3 * GT + k + 1)
                    V.tensor_scalar(tiles[k], tiles[k], mv[:, k, 0:1], rstd[:, k:k + 1], ALU.subtract,
                                    ALU.mult).then_inc(ready, 1)

            def of_tile(t, g, k):
                return t[:, bass.ds(g * GT + k, 1), :].rearrange("p a f -> p (a f)")

            def refill_ends(g, lo, hi):
                V.tensor_copy(end_ring[:, lo:hi], end_idx[:, bass.ds(g * GT + lo, hi - lo)]).then_inc(end_ready, 1)

            def node_maxima(r, g):
                for k in range(GT):
                    dve.wait_ge(row_landed[k], 16 * (r * GROUPS + g + 1))
                    dve.wait_ge(turned_out, r * TILES + g * GT + k + 1)
                    if r == 0:
                        V.tensor_tensor(work[k], rows_in[k], of_tile(hv_sb, g, k), ALU.add).then_inc(row_used, 1)
                    else:
                        V.scalar_tensor_tensor(work[k], rows_in[k], has[:, bass.ds(g * GT + k, 1)], of_tile(hv_sb, g, k),
                                               ALU.mult, ALU.add).then_inc(row_used, 1)
                    if k == CH - 1:
                        refill_ends(g + 1, 0, CH)
                    if k == GT - 1:
                        refill_ends(g + 1, CH, GT)

            for r in range(ROUNDS):
                with dve.Fori(0, TURNS) as i:
                    edge_maxima(r, i)
                join_runs(r)
                if r == 0:
                    dve.wait_ge(x_loaded, 16)
                refill_ends(0, 0, CH)
                refill_ends(0, CH, GT)
                with dve.Fori(0, GROUPS) as g:
                    node_maxima(r, g)
                    if r == 0:
                        normalise(0, g, work, lambda k: of_tile(x_sb, g, k), tile_ready)
                    if r == 2:
                        normalise(1, g, staged, lambda k: of_tile(x_sb, g, k), out_ready)

        def tile_final(eng, r, g, k):
            if r == 0:
                eng.wait_ge(tile_ready, g * GT + k + 1)
            else:
                eng.wait_ge(row_used, r * TILES + g * GT + k + 1 + GT)

        @block.sync
        def _(sp):
            sp.sem_inc(stored[0], 16)
            sp.sem_inc(stored[1], 16)
            sp.wait_ge(setup_step, CLEARS)
            for to, of in weight_loads:
                with nc.allow_non_contiguous_dma("small layouts"):
                    sp.dma_start(to, of).then_inc(w_loaded, 16)

            def write_table(r, g):
                for k in range(GT):
                    sp.wait_ge(product_out, (r * TILES) + g * GT + k + 1 + 2)
                    sp.dma_start(tables[r][bass.ds((g * GT + k) * P, P), :], staged[k]).then_inc(staged_written[k], 16)

            def store_runs(r, i):
                for h in range(2):
                    sp.wait_ge(state_done, (r * TURNS + i) * BODY + (h + 1) * HALF + 2 * BANKS)
                    sp.dma_start(runs_by_part[:, bass.ds(i * BODY + h * HALF, HALF), :],
                                 hist[:, h * HALF:(h + 1) * HALF, :]).then_inc(stored[h], 16)

            with sp.Fori(0, GROUPS) as g:
                write_table(0, g)
            sp.dma_start(x_sb[:, :, :], a["x"].rearrange("(t p) f -> p t f", p=P)).then_inc(x_loaded, 16)
            for r in range(ROUNDS):
                with sp.Fori(0, TURNS) as i:
                    store_runs(r, i)
                if r + 1 < ROUNDS:
                    with sp.Fori(0, GROUPS) as g:
                        write_table(r + 1, g)

            def write_out(g, k, rows):
                sp.wait_ge(out_ready, g * GT + k + 1)
                sp.dma_start(a["out"][bass.ds((g * GT + k) * P, rows), :],
                             staged[k][0:rows, :]).then_inc(staged_written[k], 16)

            with sp.Fori(0, GROUPS - 1) as g:
                for k in range(GT):
                    write_out(g, k, P)
            for k in range(GT):
                write_out(GROUPS - 1, k, min(P, NODES - ((GROUPS - 1) * GT + k) * P))
            for k in range(GT):
                sp.wait_ge(staged_written[k], 16 * GROUPS * (ROUNDS + 1))

        @block.gpsimd
        def _(pool):
            nc.gpsimd.iota(col_no[:, :], [[1, P]], base=0, channel_multiplier=0,
                           allow_small_or_imprecise_dtypes=True).then_inc(consts_made, 1)
            nc.gpsimd.iota(part_no[:, :], [[0, 1]], base=0, channel_multiplier=1,
                           allow_small_or_imprecise_dtypes=True).then_inc(consts_made, 1)

            with pool.Fori(0, GROUPS) as g:
                for k in range(GT):
                    pool.wait_ge(product, g * GT + k + 1)
                    pool.dma_start(xT_ring[k], a["xT"][:, bass.ds((g * GT + k) * D, D)]).then_inc(xT_landed[k], 16)

            def gather_edges(r, i):
                for c in range(NCH):
                    if c % (NCH // 2) == 0:
                        pool.wait_ge(idx_ready, (r * TURNS + i) * 2 + c // (NCH // 2) + 1)
                    pool.wait_ge(pair_summed, (r * TURNS + i) * PAIRS + (c + 1) * CH // 2)
                    pool.sem_inc(waits_met, 1)
                    for j in range(c * CH, (c + 1) * CH):
                        pool.indirect_dma_start(gath[:, j, :], None, tables[r],
                                                bass.IndirectOffsetOnAxis(idx_ring[:, j:j + 1], 0)).then_inc(gathered[c], 16)

            def join_partitions(r):
                for h in range(2):
                    pool.wait_ge(stored[h], 16 * (TURNS * (r + 1) + 1))
                if r == 0:
                    pool.wait_ge(setup_step, setup_at[SETUP_ALL])
                pool.indirect_dma_start(fix_rows[:, :], None, runs[0:SLOTS, :],
                                        bass.IndirectOffsetOnAxis(fix_from[:, 0:1], 0)).then_inc(fix_read, 16)
                pool.wait_ge(fix_joined, r + 1)
                pool.indirect_dma_start(runs, bass.IndirectOffsetOnAxis(fix_to[:, 0:1], 0), fix_rows[:, :],
                                        None).then_inc(fix_written, 16)

            def gather_nodes(r, g):
                for k in range(GT):
                    if k in (0, CH):
                        pool.wait_ge(end_ready, (r * (GROUPS + 1) + g) * 2 + (2 if k else 1))
                    pool.wait_ge(row_used, r * TILES + g * GT + k + 1)
                    pool.sem_inc(waits_met, 1)
                    pool.indirect_dma_start(rows_in[k], None, runs[0:SLOTS, :],
                                            bass.IndirectOffsetOnAxis(end_ring[:, k:k + 1], 0)).then_inc(row_landed[k], 16)

            for r in range(ROUNDS):
                for k in range(GT):
                    pool.wait_ge(staged_written[k], 16 * GROUPS * (r + 1))
                with pool.Fori(0, TURNS) as i:
                    gather_edges(r, i)
                join_partitions(r)
                pool.wait_ge(fix_written, 16 * (r + 1))
                with pool.Fori(0, GROUPS) as g:
                    gather_nodes(r, g)

        @block.scalar
        def _(act):
            act.sem_inc(turned_out, GT)
            act.sem_inc(product_out, 2)

            def keep_half(r, g, k):
                act.wait_ge(product, r * TILES + g * GT + k + 1 + GT)
                nc.scalar.copy(hv_sb[:, bass.ds(g * GT + k, 1), :].rearrange("p a f -> p (a f)"),
                               node_ps[:, k % 2, D:] if r == 0 else node_ps[:, k % 2, 0:D])

            def free_staging(r, g, k):
                act.wait_ge(staged_written[k], 16 * (r * GROUPS + g))

            def first_tiles(g, first):
                for k in range(GT):
                    keep_half(0, g, k)
                    if not first:
                        free_staging(0, g, k)
                    nc.scalar.copy(staged[k], node_ps[:, k % 2, 0:D]).then_inc(product_out, 1)

            first_tiles(0, True)
            with act.Fori(1, GROUPS) as g:
                first_tiles(g, False)

            def feed_edges(r, i):
                for c in range(NCH):
                    act.wait_ge(pair_summed, (r * TURNS + i) * PAIRS + (c + 1) * CH // 2)
                    if r > 0:
                        act.dma_start(he_sb[:, c, :], a["he"][:, bass.ds((i * NCH + c) * (CH // 2) * P, CH // 2 * P)]
                                      ).then_inc(he_loaded[c], 16)
                    if c % 2 == 1:
                        j = (c - 1) * CH
                        nc.scalar.copy(idx_ring[:, j:j + 2 * CH], src_sb[:, bass.ds(i * BODY + j, 2 * CH)]
                                       ).then_inc(idx_ready, 1)

            def turn_out(r, g, k):
                act.wait_ge(turned_ps, r * TILES + g * GT + k + 1)
                nc.scalar.copy(turned[k], turn_ps[:, k % 2, 0:D]).then_inc(turned_out, 1)

            def node_tiles(r, g):
                if r == 0:
                    for k in range(GT):
                        act.wait_ge(row_used, r * TILES + g * GT + k + 1 + GT)
                        nc.scalar.activation(work[k], work[k], ACT.Relu,
                                             scale=has[:, bass.ds(g * GT + k, 1)]).then_inc(relu_done, 1)
                    deviations(0, g)
                for k in range(GT):
                    tile_final(act, r, g, k)
                    keep_in = x_sb if r == 0 else hv_sb
                    if r < 2:
                        nc.scalar.copy(keep_in[:, bass.ds(g * GT + k, 1), :].rearrange("p a f -> p (a f)"), work[k])
                    turn_out(r, g, k)
                for k in range(GT):
                    if r == 0:
                        keep_half(1, g, k)
                    act.wait_ge(product, (r + 1) * TILES + g * GT + k + 1 + GT)
                    free_staging(r + 1, g, k)
                    if r < 2:
                        table_half = node_ps[:, k % 2, D:] if r == 0 else node_ps[:, k % 2, 0:D]
                        nc.scalar.copy(staged[k], table_half).then_inc(product_out, 1)
                    else:
                        nc.scalar.activation(staged[k], node_ps[:, k % 2, 0:D], ACT.Relu).then_inc(product_out, 1)
                if r == 2:
                    deviations(1, g)

            def deviations(n, g):
                for k in range(GT):
                    act.wait_ge(norm_step, NORM * ((n * GROUPS + g) * GT) + 2 * GT + k + 1)
                    nc.scalar.activation(std[:, k:k + 1], mv[:, k, 1:2], ACT.Sqrt,
                                         bias=eps_col[:, 0:1]).then_inc(std_ready, 1)

            for r in range(ROUNDS):
                with act.Fori(0, TURNS) as i:
                    feed_edges(r, i)
                with act.Fori(0, GROUPS) as g:
                    node_tiles(r, g)

        @block.tensor
        def _(pe):
            T = nc.tensor
            pe.sem_inc(pair_summed, PAIRS)
            pe.sem_inc(product, GT)

            def products(r, g, k, left, right, width, bias):
                t = r * TILES + g * GT + k
                pe.wait_ge(product_out, t + 2 if k == 0 else t + 1)
                bank = node_ps[:, k % 2, 0:width]
                for h in range(KH):
                    T.matmul(bank, left[:, h * P:(h + 1) * P], right[:, h, 0:width], start=(h == 0), stop=False)
                T.matmul(bank, ones_bf[:, :], b_parts[bias][:, 0:width], start=False, stop=True).then_inc(product, 1)

            pe.wait_ge(setup_step, setup_at[BIAS0_READY])
            with pe.Fori(0, GROUPS) as g:
                for k in range(GT):
                    pe.wait_ge(xT_landed[k], 16 * g + 16)
                    products(0, g, k, xT_ring[k], w_conv, 2 * D, 0)

            pe.wait_ge(setup_step, setup_at[IN_COLS_READY])
            for m in range(KH):
                for h in range(KH):
                    T.matmul(turn_ps[:, m, 0:D], w_inT[:, h, m * P:(m + 1) * P], w_n0[:, h, :], start=(h == 0),
                             stop=(h == KH - 1))
            for h in range(KH):
                last = T.matmul(turn_ps[:, 0, D:], b_in_cols[:, h, :], w_n0[:, h, :], start=(h == 0), stop=(h == KH - 1))
            last.then_inc(setup_mm, 1)

            def pick(q):
                pe.wait_ge(query, QSTEPS * q + 3)
                for lo, hi in ((0, 2 * D), (2 * D, STEPS + 1)):
                    last = T.matmul(query_ps[:, lo:hi], onehot[:, :], dst_f[:, lo:hi], start=True, stop=True)
                last.then_inc(dst_rows, 1)

            pe.wait_ge(product_out, TILES + 2)
            pick(0)

            def messages(r, i):
                for c in range(NCH):
                    if r > 0:
                        pe.wait_ge(he_loaded[c], 16 * ((r - 1) * TURNS + i + 1))
                    for q in range(c * CH // 2, (c + 1) * CH // 2):
                        pe.wait_ge(state_done, ((r * TURNS + i) * PAIRS + q + 1) * 2)
                        bank = edge_ps[:, q % BANKS, :]
                        if r > 0:
                            at = (q % (CH // 2)) * P
                            T.matmul(bank, he_sb[:, c, at:at + P], w_e[r - 1][:, :], start=True, stop=False)
                        if q == c * CH // 2:
                            pe.wait_ge(gathered[c], 16 * CH * (r * TURNS + i + 1))
                        T.matmul(bank, ident[:, :], gath[:, 2 * q:2 * q + 2, :].rearrange("p s f -> p (s f)"),
                                 start=(r == 0), stop=True).then_inc(pair_summed, 1)
                if r == 0:
                    pick(i + 1)

            def turn(r, g, k):
                tile_final(pe, r, g, k)
                t = r * TILES + g * GT + k
                pe.wait_ge(turned_out, t + GT if k == 0 else t + GT - 1)
                for h in range(KH):
                    last = T.transpose(turn_ps[:, k % 2, h * P:(h + 1) * P], work[k][:, h * P:(h + 1) * P], ident[:, :])
                last.then_inc(turned_ps, 1)

            for r in range(ROUNDS):
                with pe.Fori(0, TURNS) as i:
                    messages(r, i)
                pe.wait_ge(state_done, (r + 1) * STEPS + 2 * BANKS)
                for h in range(KH):
                    last = T.transpose(turn_ps[:, 0, h * P:(h + 1) * P], hist[:, BODY - 1, h * P:(h + 1) * P], ident[:, :])
                last.then_inc(fix_turned, 1)
                pe.wait_ge(fix_scanned, KH * (r + 1))
                for h in range(KH):
                    last = T.transpose(turn_ps[:, 1, h * P:(h + 1) * P], fix_T[:, h, :], ident[:, :])
                last.then_inc(fix_back, 1)
                if r == 0:
                    pe.wait_ge(setup_step, setup_at[SETUP_ALL])
                right, width = ((w_in, 2 * D), (w_n1, D), (w_ro, D))[r]
                with pe.Fori(0, GROUPS) as g:
                    for k in range(GT):
                        turn(r, g, k)
                    for k in range(GT):
                        pe.wait_ge(turned_out, r * TILES + g * GT + k + 1 + GT)
                        products(r + 1, g, k, turned[k], right, width, r + 1)


def kernel(x, src, dst, edge_attr_64, L0_gnn_theta_w, L0_gnn_theta_b, L0_gnn_phi_w, L0_gnn_phi_b, L1_gnn_W_in,
           L1_gnn_b_in, L1_gnn_W_u0, L1_gnn_b_u0, L1_gnn_W_u1, L1_gnn_b_u1, L1_gnn_W_ro, L1_gnn_b_ro):
    import numpy as np
    import concourse.bacc as bacc
    from concourse.bass_utils import run_bass_kernel_spmd

    def pad(v, n, fill=0):
        v = np.asarray(v)
        return np.concatenate([v, np.full((n - v.shape[0],) + v.shape[1:], fill, v.dtype)])

    x_pad = pad(x, NPAD)
    dst_pad = pad(dst, SLOTS, NPAD).reshape(P, STEPS)
    he = pad(edge_attr_64, SLOTS).reshape(P, STEPS // 2, 2, ED)
    arrays = {
        "x": x_pad,
        "xT": x_pad.reshape(TILES, P, KH, P).transpose(3, 0, 2, 1).reshape(P, TILES * D),
        "src": pad(src, SLOTS).reshape(P, STEPS),
        "dst": dst_pad,
        "dst_last": dst_pad[:, STEPS - 1],
        "he": he.transpose(2, 3, 1, 0).reshape(P, STEPS // 2 * P),
        "theta_wT": np.asarray(L0_gnn_theta_w).T, "theta_b": L0_gnn_theta_b,
        "phi_wT": np.asarray(L0_gnn_phi_w).T, "phi_b": L0_gnn_phi_b,
        "W_in": L1_gnn_W_in, "W_inT": np.asarray(L1_gnn_W_in).T, "b_in": L1_gnn_b_in,
        "W_u0": L1_gnn_W_u0, "b_u0": L1_gnn_b_u0, "W_u1": L1_gnn_W_u1, "b_u1": L1_gnn_b_u1,
        "W_ro": L1_gnn_W_ro, "b_ro": L1_gnn_b_ro,
    }
    nc = bacc.Bacc("TRN2", target_bir_lowering=False, num_devices=1)
    given, aps = {}, {}
    for name, v in arrays.items():
        v = np.ascontiguousarray(v)
        given[f"in_{name}"] = v
        aps[name] = nc.dram_tensor(f"in_{name}", v.shape, mybir.dt.from_np(v.dtype), kind="ExternalInput").ap()
    aps["out"] = nc.dram_tensor("out_nodes", [NODES, D], mybir.dt.float32, kind="ExternalOutput").ap()
    gnn_kernel(nc, aps)
    return run_bass_kernel_spmd(nc, [given], core_ids=[0]).results[0]["out_nodes"]
```

```python
import concourse.bass as bass
from concourse import mybir
from concourse.alu_op_type import AluOpType as ALU
from contextlib import ExitStack

P = 128
NODES, EDGES, D, ED = 6250, 100000, 256, 64
KH = D // P
BODY = 16
TURNS = -(-EDGES // (P * BODY))
STEPS = TURNS * BODY
SLOTS = P * STEPS
CH = 4
NCH = BODY // CH
PAIRS = BODY // 2
BANKS = 4
HALF = BODY // 2
TILES = -(-NODES // P)
GT = 7
GROUPS = TILES // GT
NPAD = TILES * P
ROUNDS = 3
EPS = 1e-5
LOWEST = -3.0e38
FAR = 1 << 20
NONE_LOW, NONE_ZERO, SPARE = SLOTS, SLOTS + 1, SLOTS + 2
QSTEPS = 12
NORM_STEPS = 3 * GT + 2
CONV, IN, NEXT0, NEXT1, OUT = range(5)
assert GROUPS * GT == TILES and TURNS == TILES


def gnn_kernel(nc, a):
    f32, bf16, i32 = mybir.dt.float32, mybir.dt.bfloat16, mybir.dt.int32
    ACT = mybir.ActivationFunctionType

    tables = [nc.dram_tensor(f"table{r}", [NPAD, D], f32, kind="Internal").ap() for r in range(ROUNDS)]
    runs = nc.dram_tensor("runs", [SPARE + P, D], f32, kind="Internal").ap()
    runs_by_part = runs[0:SLOTS, :].rearrange("(p t) f -> p t f", p=P)
    x1T = nc.dram_tensor("x1T", [P, TILES * D], f32, kind="Internal").ap()
    halves = lambda w: w.rearrange("(h k) o -> k h o", h=KH)

    ctx = ExitStack()
    with ctx:
        def sb(name, shape, dt=f32):
            return ctx.enter_context(nc.sbuf_tensor(name, shape, dt))

        def sem(name):
            return ctx.enter_context(nc.semaphore(name))

        x_sb = sb("x_sb", [P, TILES, D])
        hv_sb = sb("hv_sb", [P, TILES, D])
        gath = sb("gath", [P, BODY, D])
        hist = sb("hist", [P, BODY, D])
        he_sb = sb("he_sb", [P, NCH, CH // 2 * P])
        src_sb = sb("src_sb", [P, STEPS], i32)
        dst_i = sb("dst_i", [P, STEPS], i32)
        dst_f = sb("dst_f", [P, STEPS + 1])
        keep = sb("keep", [P, STEPS])
        lift = sb("lift", [P, STEPS])
        idx_ring = sb("idx_ring", [P, BODY], i32)
        end_low = sb("end_low", [P, TILES], i32)
        end_zero = sb("end_zero", [P, TILES], i32)
        fix_from = sb("fix_from", [P, 1], i32)
        fix_to = sb("fix_to", [P, 1], i32)
        fix_rows = sb("fix_rows", [P, D])
        fix_T = sb("fix_T", [P, KH, P])
        lastrow = sb("lastrow", [P, P])
        lastrow_i = sb("lastrow_i", [P, P], i32)
        joins = sb("joins", [P, P])
        joins_lift = sb("joins_lift", [P, P])
        w_theta = sb("w_theta", [P, KH, D])
        w_phi = sb("w_phi", [P, KH, D])
        w_diff = sb("w_diff", [P, KH, D])
        w_in = sb("w_in", [P, KH, D])
        w_inT = sb("w_inT", [P, KH, D])
        w_n0 = sb("w_n0", [P, KH, D])
        w_in_n0 = sb("w_in_n0", [P, KH, D])
        w_n1 = sb("w_n1", [P, KH, D])
        w_ro = sb("w_ro", [P, KH, D])
        w_e = [sb(f"w_e{r}", [P, 2 * D]) for r in range(2)]
        b_in_col = sb("b_in_col", [P, KH])
        b_in_cols = sb("b_in_cols", [P, KH, P])
        b_full = sb("b_full", [P, 5, D])
        b_add = sb("b_add", [P, D])
        b_parts = sb("b_parts", [P, 5, D], bf16)
        rest = sb("rest", [P, 5, D])
        part = [sb(f"part{n}", [P, 5, D], bf16) for n in range(3)]
        row_is = sb("row_is", [P, 3])
        ones_bf = sb("ones_bf", [P, P], bf16)
        none_rows = sb("none_rows", [1, 2 * D])
        ident = sb("ident", [P, P])
        col_no = sb("col_no", [P, P])
        part_no = sb("part_no", [P, 1])
        node_no = sb("node_no", [P, 1])
        bounds = sb("bounds", [P, 2])
        next_i = sb("next_i", [P, 2], i32)
        next_f = sb("next_f", [P, 2])
        onehot = sb("onehot", [P, P])
        above = sb("above", [P, P])
        junk = sb("junk", [P, STEPS])
        counts = sb("counts", [P, 3])
        found = sb("found", [P, 4])
        at_end = sb("at_end", [P, 4])
        back_T = sb("back_T", [P, D])
        stats = sb("stats", [P, GT, nc.vector.BN_STATS_DIM])
        mv = sb("mv", [P, GT, nc.vector.BN_AGGR_DIM])
        std = sb("std", [P, GT])
        rstd = sb("rstd", [P, GT])
        shift = sb("shift", [P, GT])
        eps_col = sb("eps_col", [P, 1])

        work = [gath[:, k, :] for k in range(GT)]
        xT_ring = [gath[:, GT + k, :] for k in range(GT)]
        turned = [hist[:, k, :] for k in range(GT)]
        staged = [hist[:, GT + k, :] for k in range(GT)]
        assert 2 * GT < BODY

        edge_ps = ctx.enter_context(nc.psum_tensor("edge_ps", [P, BANKS, 2 * D], f32))
        side_ps = ctx.enter_context(nc.psum_tensor("side_ps", [P, 4, 2 * D], f32))
        product_ps = [edge_ps[:, k // 2, (k % 2) * D:(k % 2 + 1) * D] for k in range(GT)]
        turned_ps = [side_ps[:, k // 2, (k % 2) * D:(k % 2 + 1) * D] for k in range(GT)]
        tile_pairs = [(k, min(k + 2, GT)) for k in range(0, GT, 2)]
        pair_end = [min(k - k % 2 + 2, GT) for k in range(GT)]
        query_ps = side_ps[:, 0:2, :].rearrange("p b f -> p (b f)")
        back_ps = side_ps[:, 2, 0:D]

        cleared = sem("cleared")
        conv_loaded = sem("conv_loaded")
        w_loaded = sem("w_loaded")
        x_loaded = sem("x_loaded")
        none_written = sem("none_written")
        consts_made = sem("consts_made")
        setup_step = sem("setup_step")
        weights_mult = sem("weights_mult")
        xT_landed = [sem(f"xT_landed{k}") for k in range(GT)]
        staged_written = sem("staged_written")
        waits_met = sem("waits_met")
        idx_ready = sem("idx_ready")
        gathered = [sem(f"gathered{c}") for c in range(NCH)]
        he_loaded = [sem(f"he_loaded{c}") for c in range(NCH)]
        pair_summed = sem("pair_summed")
        state_done = sem("state_done")
        stored = [sem(f"stored{h}") for h in range(2)]
        query = sem("query")
        dst_rows = sem("dst_rows")
        back_loaded = sem("back_loaded")
        back_product = sem("back_product")
        back_kept = sem("back_kept")
        fix_turned = sem("fix_turned")
        fix_scanned = sem("fix_scanned")
        fix_back = sem("fix_back")
        fix_read = sem("fix_read")
        fix_joined = sem("fix_joined")
        fix_written = sem("fix_written")
        row_landed = [sem(f"row_landed{k}") for k in range(GT)]
        tile_made = sem("tile_made")
        norm_step = sem("norm_step")
        std_ready = sem("std_ready")
        normed = sem("normed")
        x1_kept = sem("x1_kept")
        x1T_written = sem("x1T_written")
        tile_turned = sem("tile_turned")
        turned_out = sem("turned_out")
        product = sem("product")
        product_out = sem("product_out")

        conv_loads = [(w_theta[:, :, :], halves(a["theta_wT"])), (w_phi[:, :, :], halves(a["phi_wT"]))]
        weight_loads = [
            (src_sb[:, :], a["src"]), (dst_i[:, :], a["dst"]),
            (next_i[0:P - 1, 0:1], a["dst"][1:P, 0:1]), (next_i[0:P - 1, 1:2], a["dst"][1:P, STEPS - 1:STEPS]),
            (lastrow_i[:, :], a["dst_last"].partition_broadcast(P)),
            (w_inT[:, :, :], halves(a["W_inT"])), (w_n0[:, :, :], halves(a["W_u0"][0:D, :])),
            (b_in_col[:, :], a["b_in"].rearrange("(h k) -> k h", h=KH)),
            (rest[:, CONV, :], a["theta_b"].partition_broadcast(P)), (b_add[:, :], a["phi_b"].partition_broadcast(P)),
            (rest[:, NEXT0, :], a["b_u0"].partition_broadcast(P)),
            (b_full[:, IN, :], a["b_in"].partition_broadcast(P)),
            (b_full[:, NEXT1, :], a["b_u1"].partition_broadcast(P)),
            (b_full[:, OUT, :], a["b_ro"].partition_broadcast(P)),
            (w_in[:, :, :], halves(a["W_in"])), (w_n1[:, :, :], halves(a["W_u1"][0:D, :])),
            (w_ro[:, :, :], halves(a["W_ro"])),
        ] + [(w_e[r][ED * s:ED * (s + 1), D * s:D * (s + 1)], a[f"W_u{r}"][D:D + ED, :])
             for r in range(2) for s in range(2)]
        CLEARS = 3
        setup_at = {}

        def of_tile(t, g, k):
            return t[:, bass.ds(g * GT + k, 1), :].rearrange("p a f -> p (a f)")

        def of_group(t, g):
            return t[:, bass.ds(g * GT, GT), :]

        def wait_turnable(eng, r, g, k):
            if r == 0:
                eng.wait_ge(normed, g * GT + k + 1)
            else:
                eng.wait_ge(tile_made, (r - 1) * TILES + g * GT + k + 1)

        block = ctx.enter_context(nc.Block())

        @block.vector
        def _(dve):
            done = [0]
            V = nc.vector

            def after():
                dve.wait_ge(setup_step, done[0])

            def step(ins):
                ins.then_inc(setup_step, 1)
                done[0] += 1

            dve.sem_inc(state_done, 2 * BANKS)
            dve.sem_inc(query, 1)
            dve.sem_inc(back_kept, 1)
            V.memset(next_i[:, :], FAR).then_inc(cleared, 1)
            V.memset(w_e[0][:, :], 0.0).then_inc(cleared, 1)
            V.memset(w_e[1][:, :], 0.0).then_inc(cleared, 1)
            step(V.memset(none_rows[:, 0:D], LOWEST))
            step(V.memset(none_rows[:, D:], 0.0))
            setup_at["none rows"] = done[0]
            dve.wait_ge(conv_loaded, 16 * len(conv_loads))
            step(V.tensor_tensor(w_diff[:, :, :], w_phi[:, :, :], w_theta[:, :, :], ALU.subtract))
            setup_at["conv weights"] = done[0]
            step(V.memset(hist[:, BODY - 1, :], 0.0))
            step(V.memset(ones_bf[:, :], 1.0))
            step(V.memset(eps_col[:, :], EPS))
            dve.wait_ge(consts_made, 2)
            step(V.tensor_scalar(ident[:, :], col_no[:, :], part_no[:, 0:1], None, ALU.is_equal))
            for n in range(3):
                step(V.tensor_scalar(row_is[:, n:n + 1], part_no[:, :], float(n), None, ALU.is_equal))
            dve.wait_ge(w_loaded, 16 * len(weight_loads))
            for h in range(KH):
                step(V.tensor_copy(b_in_cols[:, h, :], b_in_col[:, h:h + 1].to_broadcast([P, P])))
            setup_at["b_in columns"] = done[0]

            step(V.tensor_copy(dst_f[:, 0:STEPS], dst_i[:, :]))
            step(V.tensor_scalar(dst_f[:, STEPS:], part_no[:, :], float(STEPS), None, ALU.mult))
            step(V.tensor_copy(next_f[:, :], next_i[:, :]))
            step(V.tensor_copy(lastrow[:, :], lastrow_i[:, :]))
            step(V.memset(keep[:, 0:1], 0.0))
            step(V.memset(joins[:, 0:1], 0.0))
            after()
            step(V.tensor_tensor(keep[:, 1:], dst_f[:, 1:STEPS], dst_f[:, 0:STEPS - 1], ALU.is_equal))
            step(V.tensor_tensor(joins[:, 1:], lastrow[:, 1:], lastrow[:, 0:P - 1], ALU.is_equal))
            step(V.tensor_copy(bounds[:, 0:1], dst_f[:, 0:1]))
            step(V.tensor_copy(bounds[:, 1:2], next_f[:, 0:1]))
            after()
            step(V.memset(bounds[0:1, 0:1], 0.0))
            step(V.tensor_scalar(lift[:, :], keep[:, :], 1.0, -LOWEST, ALU.subtract, ALU.mult))
            step(V.tensor_scalar(joins_lift[:, :], joins[:, :], 1.0, -LOWEST, ALU.subtract, ALU.mult))
            step(V.tensor_copy(node_no[:, :], part_no[:, :]))
            after()

            def pick_rows(q, along):
                dve.wait_ge(query, QSTEPS * q + 1)
                V.tensor_scalar(above[:, :], along, bounds[:, 0:1], None, ALU.is_ge).then_inc(query, 1)
                dve.wait_ge(query, QSTEPS * q + 2)
                V.scalar_tensor_tensor(onehot[:, :], along, bounds[:, 1:2], above[:, :], ALU.is_lt,
                                       ALU.mult).then_inc(query, 1)

            def find_ends(q, nodes, at_low, at_zero, by):
                dve.wait_ge(dst_rows, q + 1)
                n = [QSTEPS * q + 3]

                def then(ins):
                    ins.then_inc(query, 1)
                    n[0] += 1

                def earlier():
                    dve.wait_ge(query, n[0])

                then(V.tensor_scalar(junk[:, :], query_ps[:, 0:STEPS], nodes, 0.0, ALU.is_le, ALU.add,
                                     accum_out=counts[:, 0:1]))
                earlier()
                then(V.tensor_scalar(junk[:, :], query_ps[:, 0:STEPS], nodes, 0.0, ALU.is_lt, ALU.add,
                                     accum_out=counts[:, 1:2]))
                then(V.tensor_scalar(counts[:, 2:3], counts[:, 0:1], query_ps[:, STEPS:STEPS + 1], -1.0, ALU.add, ALU.add))
                earlier()
                then(V.tensor_tensor(found[:, 0:1], counts[:, 0:1], counts[:, 1:2], ALU.is_gt))
                for m, (none, at) in enumerate(((NONE_LOW, at_low), (NONE_ZERO, at_zero))):
                    then(V.tensor_scalar(found[:, 1 + m:2 + m], counts[:, 2:3], float(none), None, ALU.subtract))
                earlier()
                for m, (none, at) in enumerate(((NONE_LOW, at_low), (NONE_ZERO, at_zero))):
                    then(V.tensor_scalar(at, found[:, 1 + m:2 + m], found[:, 0:1], float(none), ALU.mult, ALU.add))
                then(V.tensor_scalar(bounds[:, :], bounds[:, :], by, None, ALU.subtract))
                then(V.tensor_scalar(node_no[:, :], node_no[:, :], by, None, ALU.add))

            pick_rows(0, lastrow[:, :])
            find_ends(0, dst_f[:, STEPS - 1:STEPS], at_end[:, 0:1], at_end[:, 1:2], 0.0)
            dve.wait_ge(query, QSTEPS + 1)
            step(V.tensor_copy(fix_from[:, :], at_end[:, 0:1]))
            step(V.tensor_tensor(at_end[:, 2:3], dst_f[:, STEPS - 1:STEPS], next_f[:, 1:2], ALU.not_equal))
            step(V.tensor_scalar(at_end[:, 3:4], part_no[:, :], float(SPARE), None, ALU.add))
            after()
            step(V.tensor_tensor(at_end[:, 0:1], at_end[:, 0:1], at_end[:, 3:4], ALU.subtract))
            after()
            step(V.scalar_tensor_tensor(fix_to[:, :], at_end[:, 0:1], at_end[:, 2:3], at_end[:, 3:4], ALU.mult, ALU.add))
            setup_at["rows to fix"] = done[0]

            dve.wait_ge(weights_mult, 1)
            step(V.tensor_copy(w_in_n0[:, :, :], side_ps[:, 2:4, 0:D]))
            step(V.tensor_tensor(b_full[:, NEXT0, :], side_ps[:, 2, D:], rest[:, NEXT0, :], ALU.add))
            step(V.tensor_tensor(b_full[:, CONV, :], rest[:, CONV, :], b_add[:, :], ALU.add))
            after()
            step(V.tensor_copy(part[0][:, :, :], b_full[:, :, :]))
            after()
            step(V.tensor_tensor(rest[:, :, :], b_full[:, :, :], part[0][:, :, :], ALU.subtract))
            after()
            step(V.tensor_copy(part[1][:, :, :], rest[:, :, :]))
            after()
            step(V.tensor_tensor(rest[:, :, :], rest[:, :, :], part[1][:, :, :], ALU.subtract))
            after()
            step(V.tensor_copy(part[2][:, :, :], rest[:, :, :]))
            step(V.tensor_scalar(b_parts[:, :, :], part[0][:, :, :], row_is[:, 0:1], None, ALU.mult))
            for m in (1, 2):
                after()
                step(V.scalar_tensor_tensor(b_parts[:, :, :], part[m][:, :, :], row_is[:, m:m + 1], b_parts[:, :, :],
                                            ALU.mult, ALU.add))
            setup_at["all"] = done[0]

            def edge_maxima(r, i):
                for j in range(BODY):
                    if r == 0 and j == HALF:
                        pick_rows(i + 1, col_no[:, :])
                    if j % HALF == 0:
                        dve.wait_ge(stored[j // HALF], (r * TURNS + i + 1) * 16)
                    if j % 2 == 0:
                        dve.wait_ge(pair_summed, (r * TURNS + i) * PAIRS + j // 2 + 1 + PAIRS)
                    dve.wait_ge(state_done, (r * TURNS + i) * BODY + j + 2 * BANKS)
                    fresh = lift if r == 0 else keep
                    V.scalar_tensor_tensor(hist[:, j, :], hist[:, (j - 1) % BODY, :], fresh[:, bass.ds(i * BODY + j, 1)],
                                           edge_ps[:, (j // 2) % BANKS, (j % 2) * D:(j % 2 + 1) * D],
                                           ALU.add if r == 0 else ALU.mult, ALU.max).then_inc(state_done, 1)
                if r == 0:
                    find_ends(i + 1, node_no[:, 0:1], end_low[:, bass.ds(i, 1)], end_zero[:, bass.ds(i, 1)], float(P))
                if r < 2:
                    dve.wait_ge(back_product, r * TILES + i + 2)
                    V.tensor_copy(hv_sb[:, bass.ds(i, 1), :].rearrange("p a f -> p (a f)"), back_ps).then_inc(back_kept, 1)

            def join_runs(r):
                dve.wait_ge(fix_turned, r + 1)
                for h in range(KH):
                    V.tensor_tensor_scan(fix_T[:, h, :], (joins_lift if r == 0 else joins)[:, :],
                                         side_ps[:, 0, h * P:(h + 1) * P], 0.0,
                                         ALU.add if r == 0 else ALU.mult, ALU.max).then_inc(fix_scanned, 1)
                dve.wait_ge(fix_back, r + 1)
                dve.wait_ge(fix_read, 16 * (r + 1))
                V.tensor_tensor(fix_rows[:, :], side_ps[:, 1, 0:D], fix_rows[:, :], ALU.max).then_inc(fix_joined, 1)

            def norm_factors(n, g, tiles, summed):
                base = NORM_STEPS * (n * GROUPS + g)
                for k in range(GT):
                    summed(k).then_inc(norm_step, 1)
                    dve.wait_ge(norm_step, base + 2 * k + 1)
                    V.bn_stats(stats[:, k, :], tiles[k]).then_inc(norm_step, 1)
                dve.wait_ge(norm_step, base + 2 * GT)
                dve.sem_inc(waits_met, 1)
                for k in range(GT):
                    V.bn_aggr(mv[:, k, :], stats[:, k, :]).then_inc(norm_step, 1)
                dve.wait_ge(std_ready, n * GROUPS + g + 1)
                V.reciprocal(rstd[:, :], std[:, :]).then_inc(norm_step, 1)
                dve.wait_ge(norm_step, base + 3 * GT + 1)
                V.scalar_tensor_tensor(shift[:, :], mv[:, :, 0:1].rearrange("p k o -> p (k o)"), -1.0, rstd[:, :], ALU.mult,
                                       ALU.mult).then_inc(norm_step, 1)

            def conv_sums(g):
                def summed(k):
                    dve.wait_ge(row_landed[k], 16 * (g + 1))
                    dve.wait_ge(turned_out, g * GT + k + 1)
                    if k == 0:
                        dve.wait_ge(x1_kept, 16 * (g + 1))
                    return V.scalar_tensor_tensor(work[k], of_tile(hv_sb, g, k), 0.0, of_tile(x_sb, g, k), ALU.max, ALU.add)
                norm_factors(0, g, work, summed)

            def copy_tiles(r, g):
                for k in range(GT):
                    dve.wait_ge(row_landed[k], 16 * (r * GROUPS + g + 1))
                    dve.wait_ge(turned_out, r * TILES + g * GT + k + 1)
                    V.tensor_copy(work[k], of_tile(hv_sb, g, k)).then_inc(tile_made, 1)

            def out_sums(g):
                def summed(k):
                    dve.wait_ge(product, ROUNDS * TILES + g * GT + pair_end[k] + GT)
                    if k == 0:
                        dve.wait_ge(staged_written, 16 * (ROUNDS * GROUPS + g))
                    return V.scalar_tensor_tensor(staged[k], product_ps[k], 0.0, of_tile(x_sb, g, k), ALU.max, ALU.add)
                norm_factors(1, g, staged, summed)

            for r in range(ROUNDS):
                with dve.Fori(0, TURNS) as i:
                    edge_maxima(r, i)
                join_runs(r)
                if r == 0:
                    dve.wait_ge(x_loaded, 16)
                    with dve.Fori(0, GROUPS) as g:
                        conv_sums(g)
                if r == 1:
                    with dve.Fori(0, GROUPS) as g:
                        copy_tiles(1, g)
                if r == 2:
                    copy_tiles(2, 0)
                    with dve.Fori(0, GROUPS - 1) as g:
                        copy_tiles(2, g + 1)
                        out_sums(g)
                    out_sums(GROUPS - 1)

        @block.sync
        def _(sp):
            for h in range(2):
                sp.sem_inc(stored[h], 16)
            sp.sem_inc(x1_kept, 16)
            sp.sem_inc(x1T_written, 16)
            for to, of in conv_loads:
                sp.dma_start(to, of).then_inc(conv_loaded, 16)
            sp.wait_ge(cleared, CLEARS)
            for to, of in weight_loads:
                with nc.allow_non_contiguous_dma("small layouts"):
                    sp.dma_start(to, of).then_inc(w_loaded, 16)

            def write_table(r, g):
                sp.wait_ge(product_out, (r * GROUPS + g + 1) * GT + GT)
                sp.dma_start(tables[r][bass.ds(g * GT * P, GT * P), :].rearrange("(k p) f -> p k f", p=P),
                             hist[:, GT:2 * GT, :]).then_inc(staged_written, 16)

            def store_runs(r, i):
                for h in range(2):
                    sp.wait_ge(state_done, (r * TURNS + i) * BODY + (h + 1) * HALF + 2 * BANKS)
                    sp.dma_start(runs_by_part[:, bass.ds(i * BODY + h * HALF, HALF), :],
                                 hist[:, h * HALF:(h + 1) * HALF, :]).then_inc(stored[h], 16)

            def keep_x1(g):
                sp.wait_ge(normed, (g + 1) * GT)
                sp.dma_start(of_group(x_sb, g), gath[:, 0:GT, :]).then_inc(x1_kept, 16)
                sp.wait_ge(turned_out, (g + 1) * GT + GT)
                sp.dma_start(x1T[:, bass.ds(g * GT * D, GT * D)],
                             hist[:, 0:GT, :].rearrange("p k f -> p (k f)")).then_inc(x1T_written, 16)

            with sp.Fori(0, GROUPS) as g:
                write_table(0, g)
            sp.wait_ge(setup_step, setup_at["none rows"])
            sp.dma_start(runs[NONE_LOW:NONE_ZERO + 1, :].rearrange("a f -> (a f)").unsqueeze(0),
                         none_rows[:, :]).then_inc(none_written, 16)
            sp.dma_start(x_sb[:, :, :], a["x"].rearrange("(t p) f -> p t f", p=P)).then_inc(x_loaded, 16)
            with sp.Fori(0, TURNS) as i:
                store_runs(0, i)
            with sp.Fori(0, GROUPS) as g:
                keep_x1(g)
                write_table(1, g)
            with sp.Fori(0, TURNS) as i:
                store_runs(1, i)
            with sp.Fori(0, GROUPS) as g:
                write_table(2, g)
            with sp.Fori(0, TURNS) as i:
                store_runs(2, i)
            with sp.Fori(0, GROUPS - 1) as g:
                sp.wait_ge(normed, (GROUPS + g + 1) * GT)
                sp.dma_start(a["out"][bass.ds(g * GT * P, GT * P), :].rearrange("(k p) f -> p k f", p=P),
                             hist[:, GT:2 * GT, :]).then_inc(staged_written, 16)
            first, full = (GROUPS - 1) * GT * P, GT - 1
            sp.wait_ge(normed, 2 * TILES)
            sp.dma_start(a["out"][first:first + full * P, :].rearrange("(k p) f -> p k f", p=P),
                         hist[:, GT:GT + full, :]).then_inc(staged_written, 16)
            left = NODES - first - full * P
            sp.dma_start(a["out"][NODES - left:NODES, :], staged[full][0:left, :]).then_inc(staged_written, 16)
            sp.wait_ge(staged_written, 16 * ((ROUNDS + 1) * GROUPS + 1))

        @block.gpsimd
        def _(pool):
            nc.gpsimd.iota(col_no[:, :], [[1, P]], base=0, channel_multiplier=0,
                           allow_small_or_imprecise_dtypes=True).then_inc(consts_made, 1)
            nc.gpsimd.iota(part_no[:, :], [[0, 1]], base=0, channel_multiplier=1,
                           allow_small_or_imprecise_dtypes=True).then_inc(consts_made, 1)

            with pool.Fori(0, GROUPS) as g:
                for k in range(GT):
                    pool.wait_ge(product, g * GT + k + 1)
                    pool.dma_start(xT_ring[k], a["xT"][:, bass.ds((g * GT + k) * D, D)]).then_inc(xT_landed[k], 16)

            def gather_edges(r, i):
                for c in range(NCH):
                    if c % (NCH // 2) == 0:
                        pool.wait_ge(idx_ready, (r * TURNS + i) * 2 + c // (NCH // 2) + 1)
                    pool.wait_ge(pair_summed, (r * TURNS + i) * PAIRS + (c + 1) * CH // 2)
                    pool.sem_inc(waits_met, 1)
                    for j in range(c * CH, (c + 1) * CH):
                        pool.indirect_dma_start(gath[:, j, :], None, tables[r],
                                                bass.IndirectOffsetOnAxis(idx_ring[:, j:j + 1], 0)).then_inc(gathered[c], 16)

            def join_partitions(r):
                for h in range(2):
                    pool.wait_ge(stored[h], 16 * (TURNS * (r + 1) + 1))
                if r == 0:
                    pool.wait_ge(setup_step, setup_at["rows to fix"])
                pool.indirect_dma_start(fix_rows[:, :], None, runs[0:SLOTS, :],
                                        bass.IndirectOffsetOnAxis(fix_from[:, 0:1], 0)).then_inc(fix_read, 16)
                pool.wait_ge(fix_joined, r + 1)
                pool.indirect_dma_start(runs, bass.IndirectOffsetOnAxis(fix_to[:, 0:1], 0), fix_rows[:, :],
                                        None).then_inc(fix_written, 16)

            def add_maxima(r):
                pool.wait_ge(fix_written, 16 * (r + 1))
                pool.wait_ge(back_kept, (r + 1) * TILES + 1 if r < 2 else 2 * TILES + 1)
                if r == 0:
                    pool.wait_ge(none_written, 16)
                    pool.wait_ge(query, QSTEPS * (TILES + 1) + 1)
                for t in range(TILES):
                    if t >= GT:
                        pool.wait_ge(row_landed[t % GT], 16 * (r * GROUPS + t // GT))
                    rows = (end_low if r == 0 else end_zero)[:, t:t + 1]
                    pool.indirect_dma_start(hv_sb[:, t, :], None, runs[0:SPARE, :], bass.IndirectOffsetOnAxis(rows, 0),
                                            compute_op=ALU.add).then_inc(row_landed[t % GT], 16)

            for r in range(ROUNDS):
                pool.wait_ge(staged_written, 16 * GROUPS * (r + 1))
                with pool.Fori(0, TURNS) as i:
                    gather_edges(r, i)
                join_partitions(r)
                add_maxima(r)

        @block.scalar
        def _(act):
            act.sem_inc(turned_out, GT)
            act.sem_inc(product_out, GT)

            def stage(r, g):
                for k, end in tile_pairs:
                    act.wait_ge(product, r * TILES + g * GT + end + GT)
                    if k == 0 and not (r == 0 and isinstance(g, int)):
                        act.wait_ge(staged_written, 16 * (r * GROUPS + g))
                    nc.scalar.copy(hist[:, GT + k:GT + end, :].rearrange("p k f -> p (k f)"),
                                   edge_ps[:, k // 2, 0:(end - k) * D]).then_inc(product_out, end - k)

            def feed_edges(r, i):
                for c in range(NCH):
                    act.wait_ge(pair_summed, (r * TURNS + i) * PAIRS + (c + 1) * CH // 2)
                    if r > 0:
                        act.dma_start(he_sb[:, c, :], a["he"][:, bass.ds((i * NCH + c) * (CH // 2) * P, CH // 2 * P)]
                                      ).then_inc(he_loaded[c], 16)
                    if c % 2 == 1:
                        j = (c - 1) * CH
                        nc.scalar.copy(idx_ring[:, j:j + 2 * CH], src_sb[:, bass.ds(i * BODY + j, 2 * CH)]
                                       ).then_inc(idx_ready, 1)
                if r < 2:
                    act.wait_ge(back_product, r * TILES + i + 1)
                    act.dma_start(back_T[:, :], (a["xT"] if r == 0 else x1T)[:, bass.ds(i * D, D)]).then_inc(back_loaded, 16)

            def turn_out(r, g):
                for k, end in tile_pairs:
                    act.wait_ge(tile_turned, r * TILES + g * GT + end)
                    act.wait_ge(product, r * TILES + g * GT + end + GT)
                    if r == 0 and k == 0:
                        act.wait_ge(x1T_written, 16 * (g + 1))
                    nc.scalar.copy(hist[:, k:end, :].rearrange("p k f -> p (k f)"),
                                   side_ps[:, k // 2, 0:(end - k) * D]).then_inc(turned_out, end - k)

            def layer_norm(n, g, tiles):
                act.wait_ge(norm_step, NORM_STEPS * (n * GROUPS + g) + 3 * GT)
                nc.scalar.activation(std[:, :], mv[:, :, 1:2].rearrange("p k o -> p (k o)"), ACT.Sqrt,
                                     bias=eps_col[:, 0:1]).then_inc(std_ready, 1)
                act.wait_ge(norm_step, NORM_STEPS * (n * GROUPS + g + 1))
                for k in range(GT):
                    nc.scalar.activation(tiles[k], tiles[k], ACT.Identity, bias=shift[:, k:k + 1],
                                         scale=rstd[:, k:k + 1]).then_inc(normed, 1)

            stage(0, 0)
            with act.Fori(1, GROUPS) as g:
                stage(0, g)
            act.wait_ge(w_loaded, 16 * len(weight_loads))
            with act.Fori(0, TURNS) as i:
                feed_edges(0, i)
            layer_norm(0, 0, work)
            turn_out(0, 0)
            with act.Fori(1, GROUPS) as g:
                layer_norm(0, g, work)
                stage(1, g - 1)
                turn_out(0, g)
            stage(1, GROUPS - 1)
            act.wait_ge(x1T_written, 16 * (GROUPS + 1))
            with act.Fori(0, TURNS) as i:
                feed_edges(1, i)
            with act.Fori(0, GROUPS) as g:
                turn_out(1, g)
                stage(2, g)
            with act.Fori(0, TURNS) as i:
                feed_edges(2, i)
            turn_out(2, 0)
            with act.Fori(0, GROUPS - 1) as g:
                turn_out(2, g + 1)
                layer_norm(1, g, staged)
            layer_norm(1, GROUPS - 1, staged)

        @block.tensor
        def _(pe):
            T = nc.tensor
            pe.sem_inc(pair_summed, PAIRS)
            pe.sem_inc(product, GT)
            pe.sem_inc(back_product, 1)

            def linear(to, left, right, bias=None):
                for h in range(KH):
                    last = T.matmul(to, left[:, h * P:(h + 1) * P], right[:, h, :], start=(h == 0),
                                    stop=(bias is None and h == KH - 1))
                if bias is not None:
                    last = T.matmul(to, ones_bf[:, :], b_parts[:, bias, :], start=False, stop=True)
                return last

            pe.wait_ge(setup_step, setup_at["conv weights"])
            with pe.Fori(0, GROUPS) as g:
                for k in range(GT):
                    pe.wait_ge(xT_landed[k], 16 * g + 16)
                    pe.wait_ge(product_out, g * GT + pair_end[k])
                    linear(product_ps[k], xT_ring[k], w_diff).then_inc(product, 1)

            def pick(q):
                pe.wait_ge(query, QSTEPS * q + 3)
                for lo, hi in ((0, 2 * D), (2 * D, STEPS + 1)):
                    last = T.matmul(query_ps[:, lo:hi], onehot[:, :], dst_f[:, lo:hi], start=True, stop=True)
                last.then_inc(dst_rows, 1)

            pick(0)
            pe.wait_ge(setup_step, setup_at["b_in columns"])
            for m in range(KH):
                for h in range(KH):
                    T.matmul(side_ps[:, 2 + m, 0:D], w_inT[:, h, m * P:(m + 1) * P], w_n0[:, h, :], start=(h == 0),
                             stop=(h == KH - 1))
            for h in range(KH):
                last = T.matmul(side_ps[:, 2, D:], b_in_cols[:, h, :], w_n0[:, h, :], start=(h == 0), stop=(h == KH - 1))
            last.then_inc(weights_mult, 1)

            def messages(r, i):
                for c in range(NCH):
                    if r > 0:
                        pe.wait_ge(he_loaded[c], 16 * ((r - 1) * TURNS + i + 1))
                    for q in range(c * CH // 2, (c + 1) * CH // 2):
                        pe.wait_ge(state_done, ((r * TURNS + i) * PAIRS + q + 1) * 2)
                        bank = edge_ps[:, q % BANKS, :]
                        if r > 0:
                            at = (q % (CH // 2)) * P
                            T.matmul(bank, he_sb[:, c, at:at + P], w_e[r - 1][:, :], start=True, stop=False)
                        if q == c * CH // 2:
                            pe.wait_ge(gathered[c], 16 * CH * (r * TURNS + i + 1))
                        T.matmul(bank, ident[:, :], gath[:, 2 * q:2 * q + 2, :].rearrange("p s f -> p (s f)"),
                                 start=(r == 0), stop=True).then_inc(pair_summed, 1)
                    if c == 1 and r < 2:
                        pe.wait_ge(back_loaded, 16 * (r * TILES + i + 1))
                        pe.wait_ge(back_kept, r * TILES + i + 1)
                        linear(back_ps, back_T, w_theta if r == 0 else w_in,
                               CONV if r == 0 else IN).then_inc(back_product, 1)
                if r == 0:
                    pick(i + 1)

            def turn(r, g):
                for k in range(GT):
                    wait_turnable(pe, r, g, k)
                    pe.wait_ge(turned_out, r * TILES + g * GT + pair_end[k])
                    for h in range(KH):
                        last = T.transpose(turned_ps[k][:, h * P:(h + 1) * P], work[k][:, h * P:(h + 1) * P], ident[:, :])
                    last.then_inc(tile_turned, 1)

            def multiply(r, g):
                for k in range(GT):
                    pe.wait_ge(turned_out, r * TILES + g * GT + k + 1 + GT)
                    if r < 2:
                        pe.wait_ge(product_out, (r + 1) * TILES + g * GT + pair_end[k])
                    elif not (isinstance(g, int) and g == 0):
                        pe.wait_ge(norm_step, NORM_STEPS * (GROUPS + g - 1) + 2 * pair_end[k] - 1)
                    linear(product_ps[k], turned[k], (w_in_n0, w_n1, w_ro)[r],
                           (NEXT0, NEXT1, OUT)[r]).then_inc(product, 1)

            for r in range(ROUNDS):
                if r == 0:
                    pe.wait_ge(setup_step, setup_at["all"])
                pe.wait_ge(product_out, (r + 1) * TILES + GT)
                with pe.Fori(0, TURNS) as i:
                    messages(r, i)
                pe.wait_ge(state_done, (r + 1) * STEPS + 2 * BANKS)
                if r == 0:
                    pe.wait_ge(query, QSTEPS * (TILES + 1) + 1)
                for h in range(KH):
                    last = T.transpose(side_ps[:, 0, h * P:(h + 1) * P], hist[:, BODY - 1, h * P:(h + 1) * P], ident[:, :])
                last.then_inc(fix_turned, 1)
                pe.wait_ge(fix_scanned, KH * (r + 1))
                for h in range(KH):
                    last = T.transpose(side_ps[:, 1, h * P:(h + 1) * P], fix_T[:, h, :], ident[:, :])
                last.then_inc(fix_back, 1)
                pe.wait_ge(fix_joined, r + 1)
                if r < 2:
                    with pe.Fori(0, GROUPS) as g:
                        turn(r, g)
                        multiply(r, g)
                else:
                    turn(2, 0)
                    multiply(2, 0)
                    with pe.Fori(1, GROUPS) as g:
                        turn(2, g)
                        multiply(2, g)


def kernel(x, src, dst, edge_attr_64, L0_gnn_theta_w, L0_gnn_theta_b, L0_gnn_phi_w, L0_gnn_phi_b, L1_gnn_W_in,
           L1_gnn_b_in, L1_gnn_W_u0, L1_gnn_b_u0, L1_gnn_W_u1, L1_gnn_b_u1, L1_gnn_W_ro, L1_gnn_b_ro):
    import numpy as np
    import concourse.bacc as bacc
    from concourse.bass_utils import run_bass_kernel_spmd

    def pad(v, n, fill=0):
        v = np.asarray(v)
        return np.concatenate([v, np.full((n - v.shape[0],) + v.shape[1:], fill, v.dtype)])

    x_pad = pad(x, NPAD)
    dst_pad = pad(dst, SLOTS, NPAD).reshape(P, STEPS)
    he = pad(edge_attr_64, SLOTS).reshape(P, STEPS // 2, 2, ED)
    arrays = {
        "x": x_pad,
        "xT": x_pad.reshape(TILES, P, KH, P).transpose(3, 0, 2, 1).reshape(P, TILES * D),
        "src": pad(src, SLOTS).reshape(P, STEPS),
        "dst": dst_pad,
        "dst_last": dst_pad[:, STEPS - 1],
        "he": he.transpose(2, 3, 1, 0).reshape(P, STEPS // 2 * P),
        "theta_wT": np.asarray(L0_gnn_theta_w).T, "theta_b": L0_gnn_theta_b,
        "phi_wT": np.asarray(L0_gnn_phi_w).T, "phi_b": L0_gnn_phi_b,
        "W_in": L1_gnn_W_in, "W_inT": np.asarray(L1_gnn_W_in).T, "b_in": L1_gnn_b_in,
        "W_u0": L1_gnn_W_u0, "b_u0": L1_gnn_b_u0, "W_u1": L1_gnn_W_u1, "b_u1": L1_gnn_b_u1,
        "W_ro": L1_gnn_W_ro, "b_ro": L1_gnn_b_ro,
    }
    nc = bacc.Bacc("TRN2", target_bir_lowering=False, num_devices=1)
    given, aps = {}, {}
    for name, v in arrays.items():
        v = np.ascontiguousarray(v)
        given[f"in_{name}"] = v
        aps[name] = nc.dram_tensor(f"in_{name}", v.shape, mybir.dt.from_np(v.dtype), kind="ExternalInput").ap()
    aps["out"] = nc.dram_tensor("out_nodes", [NODES, D], mybir.dt.float32, kind="ExternalOutput").ap()
    gnn_kernel(nc, aps)
    return run_bass_kernel_spmd(nc, [given], core_ids=[0]).results[0]["out_nodes"]
```

```python
import concourse.bass as bass
from concourse import mybir
from concourse.alu_op_type import AluOpType as ALU
from contextlib import ExitStack

P = 128
NODES, EDGES, D, ED = 6250, 100000, 256, 64
KH = D // P
BODY = 16
TURNS = -(-EDGES // (P * BODY))
STEPS = TURNS * BODY
SLOTS = P * STEPS
CH = 4
NCH = BODY // CH
PAIRS = BODY // 2
BANKS = 4
HALF = BODY // 2
TILES = -(-NODES // P)
GT = 7
GROUPS = TILES // GT
NPAD = TILES * P
ROUNDS = 3
EPS = 1e-5
LOWEST = -3.0e38
FAR = 1 << 20
NONE_LOW, NONE_ZERO, SPARE = SLOTS, SLOTS + 1, SLOTS + 2
QSTEPS = 12
NORM_STEPS = 3 * GT + 1
CONV, IN, NEXT0, NEXT1, OUT = range(5)
assert GROUPS * GT == TILES and TURNS == TILES


def gnn_kernel(nc, a):
    f32, bf16, i32 = mybir.dt.float32, mybir.dt.bfloat16, mybir.dt.int32
    ACT = mybir.ActivationFunctionType

    tables = [nc.dram_tensor(f"table{r}", [NPAD, D], f32, kind="Internal").ap() for r in range(ROUNDS)]
    runs = nc.dram_tensor("runs", [SPARE + P, D], f32, kind="Internal").ap()
    runs_by_part = runs[0:SLOTS, :].rearrange("(p t) f -> p t f", p=P)
    x1T = nc.dram_tensor("x1T", [P, TILES * D], f32, kind="Internal").ap()
    halves = lambda w: w.rearrange("(h k) o -> k h o", h=KH)

    ctx = ExitStack()
    with ctx:
        def sb(name, shape, dt=f32):
            return ctx.enter_context(nc.sbuf_tensor(name, shape, dt))

        def sem(name):
            return ctx.enter_context(nc.semaphore(name))

        x_sb = sb("x_sb", [P, TILES, D])
        hv_sb = sb("hv_sb", [P, TILES, D])
        gath = sb("gath", [P, BODY, D])
        hist = sb("hist", [P, BODY, D])
        he_sb = sb("he_sb", [P, NCH, CH // 2 * P])
        src_sb = sb("src_sb", [P, STEPS], i32)
        dst_i = sb("dst_i", [P, STEPS], i32)
        dst_f = sb("dst_f", [P, STEPS + 1])
        keep = sb("keep", [P, STEPS])
        lift = sb("lift", [P, STEPS])
        idx_ring = sb("idx_ring", [P, BODY], i32)
        end_low = sb("end_low", [P, TILES], i32)
        end_zero = sb("end_zero", [P, TILES], i32)
        fix_from = sb("fix_from", [P, 1], i32)
        fix_to = sb("fix_to", [P, 1], i32)
        fix_rows = sb("fix_rows", [P, D])
        fix_T = sb("fix_T", [P, KH, P])
        lastrow = sb("lastrow", [P, P])
        lastrow_i = sb("lastrow_i", [P, P], i32)
        joins = sb("joins", [P, P])
        joins_lift = sb("joins_lift", [P, P])
        w_theta = sb("w_theta", [P, KH, D])
        w_phi = sb("w_phi", [P, KH, D])
        w_diff = sb("w_diff", [P, KH, D])
        w_in = sb("w_in", [P, KH, D])
        w_inT = sb("w_inT", [P, KH, D])
        w_n0 = sb("w_n0", [P, KH, D])
        w_in_n0 = sb("w_in_n0", [P, KH, D])
        w_n1 = sb("w_n1", [P, KH, D])
        w_ro = sb("w_ro", [P, KH, D])
        w_e = [sb(f"w_e{r}", [P, 2 * D]) for r in range(2)]
        b_in_col = sb("b_in_col", [P, KH])
        b_in_cols = sb("b_in_cols", [P, KH, P])
        b_full = sb("b_full", [P, 5, D])
        b_add = sb("b_add", [P, D])
        b_parts = sb("b_parts", [P, 5, D], bf16)
        rest = sb("rest", [P, 5, D])
        part = [sb(f"part{n}", [P, 5, D], bf16) for n in range(3)]
        row_is = sb("row_is", [P, 3])
        ones_bf = sb("ones_bf", [P, P], bf16)
        none_rows = sb("none_rows", [1, 2 * D])
        ident = sb("ident", [P, P])
        col_no = sb("col_no", [P, P])
        part_no = sb("part_no", [P, 1])
        node_no = sb("node_no", [P, 1])
        bounds = sb("bounds", [P, 2])
        next_i = sb("next_i", [P, 2], i32)
        next_f = sb("next_f", [P, 2])
        onehot = sb("onehot", [P, P])
        above = sb("above", [P, P])
        junk = sb("junk", [P, STEPS])
        counts = sb("counts", [P, 3])
        found = sb("found", [P, 4])
        at_end = sb("at_end", [P, 4])
        back_T = sb("back_T", [P, D])
        stats = sb("stats", [P, GT, nc.vector.BN_STATS_DIM])
        mv = sb("mv", [P, GT, nc.vector.BN_AGGR_DIM])
        std = sb("std", [P, GT])
        rstd = sb("rstd", [P, GT])
        eps_col = sb("eps_col", [P, 1])

        work = [gath[:, k, :] for k in range(GT)]
        xT_ring = [gath[:, GT + k, :] for k in range(GT)]
        normal = [gath[:, GT + k, :] for k in range(GT)]
        turned = [hist[:, k, :] for k in range(GT)]
        staged = [hist[:, GT + k, :] for k in range(GT)]
        assert 2 * GT < BODY

        edge_ps = ctx.enter_context(nc.psum_tensor("edge_ps", [P, BANKS, 2 * D], f32))
        side_ps = ctx.enter_context(nc.psum_tensor("side_ps", [P, 4, 2 * D], f32))
        product_ps = [edge_ps[:, k // 2, (k % 2) * D:(k % 2 + 1) * D] for k in range(GT)]
        turned_ps = [side_ps[:, k // 2, (k % 2) * D:(k % 2 + 1) * D] for k in range(GT)]
        tile_pairs = [(k, min(k + 2, GT)) for k in range(0, GT, 2)]
        WRITES = 16 * len(tile_pairs)
        pair_end = [min(k - k % 2 + 2, GT) for k in range(GT)]
        query_ps = side_ps[:, 0:2, :].rearrange("p b f -> p (b f)")
        back_ps = side_ps[:, 2, 0:D]

        cleared = sem("cleared")
        conv_loaded = sem("conv_loaded")
        w_loaded = sem("w_loaded")
        x_loaded = sem("x_loaded")
        none_written = sem("none_written")
        consts_made = sem("consts_made")
        setup_step = sem("setup_step")
        weights_mult = sem("weights_mult")
        xT_landed = [sem(f"xT_landed{k}") for k in range(len(tile_pairs))]
        staged_written = sem("staged_written")
        waits_met = sem("waits_met")
        idx_ready = sem("idx_ready")
        gathered = [sem(f"gathered{q}") for q in range(PAIRS)]
        he_loaded = [sem(f"he_loaded{c}") for c in range(NCH)]
        pair_summed = sem("pair_summed")
        state_done = sem("state_done")
        stored = [sem(f"stored{c}") for c in range(NCH)]
        query = sem("query")
        dst_rows = sem("dst_rows")
        back_loaded = sem("back_loaded")
        back_product = sem("back_product")
        back_kept = sem("back_kept")
        fix_turned = sem("fix_turned")
        fix_scanned = sem("fix_scanned")
        fix_back = sem("fix_back")
        fix_read = sem("fix_read")
        fix_joined = sem("fix_joined")
        fix_written = sem("fix_written")
        row_landed = [sem(f"row_landed{k}") for k in range(GT)]
        norm_step = sem("norm_step")
        std_ready = sem("std_ready")
        normed = sem("normed")
        x1_kept = sem("x1_kept")
        tile_made = sem("tile_made")
        x1T_written = sem("x1T_written")
        tile_turned = sem("tile_turned")
        turned_out = sem("turned_out")
        product = sem("product")
        product_out = sem("product_out")

        conv_loads = [(w_theta[:, :, :], halves(a["theta_wT"])), (w_phi[:, :, :], halves(a["phi_wT"]))]
        weight_loads = [
            (src_sb[:, :], a["src"]), (dst_i[:, :], a["dst"]),
            (next_i[0:P - 1, 0:1], a["dst"][1:P, 0:1]), (next_i[0:P - 1, 1:2], a["dst"][1:P, STEPS - 1:STEPS]),
            (lastrow_i[:, :], a["dst_last"].partition_broadcast(P)),
            (w_inT[:, :, :], halves(a["W_inT"])), (w_n0[:, :, :], halves(a["W_u0"][0:D, :])),
            (b_in_col[:, :], a["b_in"].rearrange("(h k) -> k h", h=KH)),
            (rest[:, CONV, :], a["theta_b"].partition_broadcast(P)), (b_add[:, :], a["phi_b"].partition_broadcast(P)),
            (rest[:, NEXT0, :], a["b_u0"].partition_broadcast(P)),
            (b_full[:, IN, :], a["b_in"].partition_broadcast(P)),
            (b_full[:, NEXT1, :], a["b_u1"].partition_broadcast(P)),
            (b_full[:, OUT, :], a["b_ro"].partition_broadcast(P)),
            (w_in[:, :, :], halves(a["W_in"])), (w_n1[:, :, :], halves(a["W_u1"][0:D, :])),
            (w_ro[:, :, :], halves(a["W_ro"])),
        ] + [(w_e[r][ED * s:ED * (s + 1), D * s:D * (s + 1)], a[f"W_u{r}"][D:D + ED, :])
             for r in range(2) for s in range(2)]
        CLEARS = 3
        setup_at = {}

        def of_tile(t, g, k):
            return t[:, bass.ds(g * GT + k, 1), :].rearrange("p a f -> p (a f)")

        def of_group(t, g):
            return t[:, bass.ds(g * GT, GT), :]

        block = ctx.enter_context(nc.Block())

        @block.vector
        def _(dve):
            done = [0]
            V = nc.vector

            def after():
                dve.wait_ge(setup_step, done[0])

            def step(ins):
                ins.then_inc(setup_step, 1)
                done[0] += 1

            dve.sem_inc(state_done, 2 * BANKS)
            dve.sem_inc(query, 1)
            dve.sem_inc(back_kept, 1)
            V.memset(next_i[:, :], FAR).then_inc(cleared, 1)
            V.memset(w_e[0][:, :], 0.0).then_inc(cleared, 1)
            V.memset(w_e[1][:, :], 0.0).then_inc(cleared, 1)
            step(V.memset(none_rows[:, 0:D], LOWEST))
            step(V.memset(none_rows[:, D:], 0.0))
            setup_at["none rows"] = done[0]
            dve.wait_ge(conv_loaded, 16 * len(conv_loads))
            step(V.tensor_tensor(w_diff[:, :, :], w_phi[:, :, :], w_theta[:, :, :], ALU.subtract))
            setup_at["conv weights"] = done[0]
            step(V.memset(hist[:, BODY - 1, :], 0.0))
            step(V.memset(ones_bf[:, :], 1.0))
            step(V.memset(eps_col[:, :], EPS))
            dve.wait_ge(consts_made, 2)
            step(V.tensor_scalar(ident[:, :], col_no[:, :], part_no[:, 0:1], None, ALU.is_equal))
            for n in range(3):
                step(V.tensor_scalar(row_is[:, n:n + 1], part_no[:, :], float(n), None, ALU.is_equal))
            dve.wait_ge(w_loaded, 16 * len(weight_loads))
            for h in range(KH):
                step(V.tensor_copy(b_in_cols[:, h, :], b_in_col[:, h:h + 1].to_broadcast([P, P])))
            setup_at["b_in columns"] = done[0]

            step(V.tensor_copy(dst_f[:, 0:STEPS], dst_i[:, :]))
            step(V.tensor_scalar(dst_f[:, STEPS:], part_no[:, :], float(STEPS), None, ALU.mult))
            step(V.tensor_copy(next_f[:, :], next_i[:, :]))
            step(V.tensor_copy(lastrow[:, :], lastrow_i[:, :]))
            step(V.memset(keep[:, 0:1], 0.0))
            step(V.memset(joins[:, 0:1], 0.0))
            after()
            step(V.tensor_tensor(keep[:, 1:], dst_f[:, 1:STEPS], dst_f[:, 0:STEPS - 1], ALU.is_equal))
            step(V.tensor_tensor(joins[:, 1:], lastrow[:, 1:], lastrow[:, 0:P - 1], ALU.is_equal))
            step(V.tensor_copy(bounds[:, 0:1], dst_f[:, 0:1]))
            step(V.tensor_copy(bounds[:, 1:2], next_f[:, 0:1]))
            after()
            step(V.memset(bounds[0:1, 0:1], 0.0))
            step(V.tensor_scalar(lift[:, :], keep[:, :], 1.0, -LOWEST, ALU.subtract, ALU.mult))
            step(V.tensor_scalar(joins_lift[:, :], joins[:, :], 1.0, -LOWEST, ALU.subtract, ALU.mult))
            step(V.tensor_copy(node_no[:, :], part_no[:, :]))
            after()

            def pick_rows(q, along):
                dve.wait_ge(query, QSTEPS * q + 1)
                V.tensor_scalar(above[:, :], along, bounds[:, 0:1], None, ALU.is_ge).then_inc(query, 1)
                dve.wait_ge(query, QSTEPS * q + 2)
                V.scalar_tensor_tensor(onehot[:, :], along, bounds[:, 1:2], above[:, :], ALU.is_lt,
                                       ALU.mult).then_inc(query, 1)

            def find_ends(q, nodes, at_low, at_zero, by):
                dve.wait_ge(dst_rows, q + 1)
                n = [QSTEPS * q + 3]

                def then(ins):
                    ins.then_inc(query, 1)
                    n[0] += 1

                def earlier():
                    dve.wait_ge(query, n[0])

                then(V.tensor_scalar(junk[:, :], query_ps[:, 0:STEPS], nodes, 0.0, ALU.is_le, ALU.add,
                                     accum_out=counts[:, 0:1]))
                earlier()
                then(V.tensor_scalar(junk[:, :], query_ps[:, 0:STEPS], nodes, 0.0, ALU.is_lt, ALU.add,
                                     accum_out=counts[:, 1:2]))
                then(V.tensor_scalar(counts[:, 2:3], counts[:, 0:1], query_ps[:, STEPS:STEPS + 1], -1.0, ALU.add, ALU.add))
                earlier()
                then(V.tensor_tensor(found[:, 0:1], counts[:, 0:1], counts[:, 1:2], ALU.is_gt))
                for m, (none, at) in enumerate(((NONE_LOW, at_low), (NONE_ZERO, at_zero))):
                    then(V.tensor_scalar(found[:, 1 + m:2 + m], counts[:, 2:3], float(none), None, ALU.subtract))
                earlier()
                for m, (none, at) in enumerate(((NONE_LOW, at_low), (NONE_ZERO, at_zero))):
                    then(V.tensor_scalar(at, found[:, 1 + m:2 + m], found[:, 0:1], float(none), ALU.mult, ALU.add))
                then(V.tensor_scalar(bounds[:, :], bounds[:, :], by, None, ALU.subtract))
                then(V.tensor_scalar(node_no[:, :], node_no[:, :], by, None, ALU.add))

            pick_rows(0, lastrow[:, :])
            find_ends(0, dst_f[:, STEPS - 1:STEPS], at_end[:, 0:1], at_end[:, 1:2], 0.0)
            dve.wait_ge(query, QSTEPS + 1)
            step(V.tensor_copy(fix_from[:, :], at_end[:, 0:1]))
            step(V.tensor_tensor(at_end[:, 2:3], dst_f[:, STEPS - 1:STEPS], next_f[:, 1:2], ALU.not_equal))
            step(V.tensor_scalar(at_end[:, 3:4], part_no[:, :], float(SPARE), None, ALU.add))
            after()
            step(V.tensor_tensor(at_end[:, 0:1], at_end[:, 0:1], at_end[:, 3:4], ALU.subtract))
            after()
            step(V.scalar_tensor_tensor(fix_to[:, :], at_end[:, 0:1], at_end[:, 2:3], at_end[:, 3:4], ALU.mult, ALU.add))
            setup_at["rows to fix"] = done[0]

            dve.wait_ge(weights_mult, 1)
            step(V.tensor_copy(w_in_n0[:, :, :], side_ps[:, 2:4, 0:D]))
            step(V.tensor_tensor(b_full[:, NEXT0, :], side_ps[:, 2, D:], rest[:, NEXT0, :], ALU.add))
            step(V.tensor_tensor(b_full[:, CONV, :], rest[:, CONV, :], b_add[:, :], ALU.add))
            after()
            step(V.tensor_copy(part[0][:, :, :], b_full[:, :, :]))
            after()
            step(V.tensor_tensor(rest[:, :, :], b_full[:, :, :], part[0][:, :, :], ALU.subtract))
            after()
            step(V.tensor_copy(part[1][:, :, :], rest[:, :, :]))
            after()
            step(V.tensor_tensor(rest[:, :, :], rest[:, :, :], part[1][:, :, :], ALU.subtract))
            after()
            step(V.tensor_copy(part[2][:, :, :], rest[:, :, :]))
            step(V.tensor_scalar(b_parts[:, :, :], part[0][:, :, :], row_is[:, 0:1], None, ALU.mult))
            for m in (1, 2):
                after()
                step(V.scalar_tensor_tensor(b_parts[:, :, :], part[m][:, :, :], row_is[:, m:m + 1], b_parts[:, :, :],
                                            ALU.mult, ALU.add))
            setup_at["all"] = done[0]

            def edge_maxima(r, i):
                for j in range(BODY):
                    if r == 0 and j == HALF:
                        pick_rows(i + 1, col_no[:, :])
                    if j % CH == 0:
                        dve.wait_ge(stored[j // CH], (r * TURNS + i + 1) * 16)
                    if j % 2 == 0:
                        dve.wait_ge(pair_summed, (r * TURNS + i) * PAIRS + j // 2 + 1 + PAIRS)
                    dve.wait_ge(state_done, (r * TURNS + i) * BODY + j + 2 * BANKS)
                    fresh = lift if r == 0 else keep
                    V.scalar_tensor_tensor(hist[:, j, :], hist[:, (j - 1) % BODY, :], fresh[:, bass.ds(i * BODY + j, 1)],
                                           edge_ps[:, (j // 2) % BANKS, (j % 2) * D:(j % 2 + 1) * D],
                                           ALU.add if r == 0 else ALU.mult, ALU.max).then_inc(state_done, 1)
                if r == 0:
                    find_ends(i + 1, node_no[:, 0:1], end_low[:, bass.ds(i, 1)], end_zero[:, bass.ds(i, 1)], float(P))
                if r < 2:
                    dve.wait_ge(back_product, r * TILES + i + 2)
                    V.tensor_copy(hv_sb[:, bass.ds(i, 1), :].rearrange("p a f -> p (a f)"), back_ps).then_inc(back_kept, 1)

            def join_runs(r):
                dve.wait_ge(fix_turned, r + 1)
                for h in range(KH):
                    V.tensor_tensor_scan(fix_T[:, h, :], (joins_lift if r == 0 else joins)[:, :],
                                         side_ps[:, 0, h * P:(h + 1) * P], 0.0,
                                         ALU.add if r == 0 else ALU.mult, ALU.max).then_inc(fix_scanned, 1)
                dve.wait_ge(fix_back, r + 1)
                dve.wait_ge(fix_read, 16 * (r + 1))
                V.tensor_tensor(fix_rows[:, :], side_ps[:, 1, 0:D], fix_rows[:, :], ALU.max).then_inc(fix_joined, 1)

            def layer_norm(n, g, tiles, summed):
                base = NORM_STEPS * (n * GROUPS + g)

                def statistics(k):
                    dve.wait_ge(norm_step, base + max(2 * k, 1))
                    V.bn_stats(stats[:, k, :], tiles[k]).then_inc(norm_step, 1)

                for k in range(GT):
                    summed(k).then_inc(norm_step, 1)
                    if k > 0:
                        statistics(k - 1)
                statistics(GT - 1)
                dve.wait_ge(norm_step, base + 2 * GT)
                dve.sem_inc(waits_met, 1)
                for k in range(GT):
                    V.bn_aggr(mv[:, k, :], stats[:, k, :]).then_inc(norm_step, 1)
                dve.wait_ge(std_ready, n * GROUPS + g + 1)
                V.reciprocal(rstd[:, :], std[:, :]).then_inc(norm_step, 1)
                dve.wait_ge(norm_step, base + 3 * GT + 1)
                if n == 0:
                    dve.wait_ge(turned_out, (g + 1) * GT)
                    if not isinstance(g, int):
                        dve.wait_ge(x1_kept, g)
                else:
                    dve.wait_ge(staged_written, WRITES * (ROUNDS * GROUPS + g))
                for k in range(GT):
                    V.tensor_scalar(normal[k], tiles[k], mv[:, k, 0:1], rstd[:, k:k + 1], ALU.subtract,
                                    ALU.mult).then_inc(normed, 1)

            def conv_sums(g):
                if not isinstance(g, int):
                    dve.wait_ge(normed, g * GT)

                def summed(k):
                    dve.wait_ge(row_landed[k], 16 * (g + 1))
                    return V.scalar_tensor_tensor(work[k], of_tile(hv_sb, g, k), 0.0, of_tile(x_sb, g, k), ALU.max, ALU.add)
                layer_norm(0, g, work, summed)

            def stage_with_bias(g):
                for k, end in tile_pairs:
                    dve.wait_ge(product, 2 * TILES + g * GT + end + GT)
                    if k == 0:
                        dve.wait_ge(staged_written, WRITES * (2 * GROUPS + g))
                    for t in range(k, end):
                        last = V.tensor_tensor(staged[t], product_ps[t], b_full[:, NEXT1, :], ALU.add)
                    last.then_inc(product_out, end - k)

            def out_sums(g):
                dve.wait_ge(normed, TILES + g * GT)
                dve.wait_ge(x1_kept, GROUPS)

                def summed(k):
                    dve.wait_ge(product, ROUNDS * TILES + g * GT + pair_end[k] + GT)
                    return V.scalar_tensor_tensor(staged[k], product_ps[k], 0.0, of_tile(x_sb, g, k), ALU.max, ALU.add)
                layer_norm(1, g, staged, summed)

            for r in range(ROUNDS):
                with dve.Fori(0, TURNS) as i:
                    edge_maxima(r, i)
                join_runs(r)
                if r == 0:
                    dve.wait_ge(x_loaded, 16 * TILES)
                    conv_sums(0)
                    with dve.Fori(1, GROUPS) as g:
                        conv_sums(g)
                if r == 1:
                    with dve.Fori(0, GROUPS) as g:
                        stage_with_bias(g)
                if r == 2:
                    with dve.Fori(0, GROUPS) as g:
                        out_sums(g)

        @block.sync
        def _(sp):
            for c in range(NCH):
                sp.sem_inc(stored[c], 16)
            sp.sem_inc(x1T_written, 16)
            for to, of in conv_loads:
                sp.dma_start(to, of).then_inc(conv_loaded, 16)
            sp.wait_ge(cleared, CLEARS)
            for to, of in weight_loads:
                with nc.allow_non_contiguous_dma("small layouts"):
                    sp.dma_start(to, of).then_inc(w_loaded, 16)

            def write_table(r, g):
                for k, end in tile_pairs:
                    sp.wait_ge(product_out, (r * GROUPS + g) * GT + end + GT)
                    sp.dma_start(tables[r][bass.ds((g * GT + k) * P, (end - k) * P), :].rearrange("(k p) f -> p k f", p=P),
                                 hist[:, GT + k:GT + end, :]).then_inc(staged_written, 16)

            def store_runs(r, i):
                if r == 0:
                    sp.dma_start(x_sb[:, bass.ds(i, 1), :].rearrange("p a f -> p (a f)"),
                                 a["x"][bass.ds(i * P, P), :]).then_inc(x_loaded, 16)
                for c in range(NCH):
                    sp.wait_ge(state_done, (r * TURNS + i) * BODY + (c + 1) * CH + 2 * BANKS)
                    sp.dma_start(runs_by_part[:, bass.ds(i * BODY + c * CH, CH), :],
                                 hist[:, c * CH:(c + 1) * CH, :]).then_inc(stored[c], 16)

            def write_x1T(g):
                sp.wait_ge(turned_out, (g + 1) * GT + GT)
                sp.dma_start(x1T[:, bass.ds(g * GT * D, GT * D)],
                             hist[:, 0:GT, :].rearrange("p k f -> p (k f)")).then_inc(x1T_written, 16)

            with sp.Fori(0, GROUPS) as g:
                write_table(0, g)
            sp.wait_ge(setup_step, setup_at["none rows"])
            sp.dma_start(runs[NONE_LOW:NONE_ZERO + 1, :].rearrange("a f -> (a f)").unsqueeze(0),
                         none_rows[:, :]).then_inc(none_written, 16)
            with sp.Fori(0, TURNS) as i:
                store_runs(0, i)
            with sp.Fori(0, GROUPS) as g:
                write_x1T(g)
                write_table(1, g)
            with sp.Fori(0, TURNS) as i:
                store_runs(1, i)
            with sp.Fori(0, GROUPS) as g:
                write_table(2, g)
            with sp.Fori(0, TURNS) as i:
                store_runs(2, i)
            def write_out(g, k, end, rows):
                sp.wait_ge(normed, (GROUPS + g) * GT + end)
                sp.dma_start(a["out"][bass.ds((g * GT + k) * P, (end - k) * P), :].rearrange("(k p) f -> p k f", p=P)
                             if rows == P else a["out"][NODES - rows:NODES, :],
                             gath[:, GT + k:GT + end, :] if rows == P else normal[k][0:rows, :]).then_inc(staged_written, 16)

            with sp.Fori(0, GROUPS - 1) as g:
                for k, end in tile_pairs:
                    write_out(g, k, end, P)
            for k, end in tile_pairs:
                write_out(GROUPS - 1, k, end, P if end < GT else NODES - (TILES - 1) * P)
            sp.wait_ge(staged_written, WRITES * GROUPS * (ROUNDS + 1))

        @block.gpsimd
        def _(pool):
            nc.gpsimd.iota(col_no[:, :], [[1, P]], base=0, channel_multiplier=0,
                           allow_small_or_imprecise_dtypes=True).then_inc(consts_made, 1)
            nc.gpsimd.iota(part_no[:, :], [[0, 1]], base=0, channel_multiplier=1,
                           allow_small_or_imprecise_dtypes=True).then_inc(consts_made, 1)

            with pool.Fori(0, GROUPS) as g:
                for k, end in tile_pairs:
                    pool.wait_ge(product, g * GT + end)
                    pool.dma_start(gath[:, GT + k:GT + end, :].rearrange("p k f -> p (k f)"),
                                   a["xT"][:, bass.ds((g * GT + k) * D, (end - k) * D)]).then_inc(xT_landed[k // 2], 16)

            def gather_edges(r, i):
                for c in range(NCH):
                    if c % (NCH // 2) == 0:
                        pool.wait_ge(idx_ready, (r * TURNS + i) * 2 + c // (NCH // 2) + 1)
                    pool.wait_ge(pair_summed, (r * TURNS + i) * PAIRS + (c + 1) * CH // 2)
                    pool.sem_inc(waits_met, 1)
                    for j in range(c * CH, (c + 1) * CH):
                        pool.indirect_dma_start(gath[:, j, :], None, tables[r],
                                                bass.IndirectOffsetOnAxis(idx_ring[:, j:j + 1], 0)).then_inc(gathered[j // 2], 16)

            def join_partitions(r):
                for c in range(NCH):
                    pool.wait_ge(stored[c], 16 * (TURNS * (r + 1) + 1))
                if r == 0:
                    pool.wait_ge(setup_step, setup_at["rows to fix"])
                pool.indirect_dma_start(fix_rows[:, :], None, runs[0:SLOTS, :],
                                        bass.IndirectOffsetOnAxis(fix_from[:, 0:1], 0)).then_inc(fix_read, 16)
                pool.wait_ge(fix_joined, r + 1)
                pool.indirect_dma_start(runs, bass.IndirectOffsetOnAxis(fix_to[:, 0:1], 0), fix_rows[:, :],
                                        None).then_inc(fix_written, 16)

            def add_maxima(r):
                pool.wait_ge(fix_written, 16 * (r + 1))
                pool.wait_ge(back_kept, (r + 1) * TILES + 1 if r < 2 else 2 * TILES + 1)
                if r == 0:
                    pool.wait_ge(none_written, 16)
                    pool.wait_ge(query, QSTEPS * (TILES + 1) + 1)
                for t in range(TILES):
                    if t >= GT:
                        pool.wait_ge(row_landed[t % GT], 16 * (r * GROUPS + t // GT))
                    rows = (end_low if r == 0 else end_zero)[:, t:t + 1]
                    pool.indirect_dma_start(hv_sb[:, t, :], None, runs[0:SPARE, :], bass.IndirectOffsetOnAxis(rows, 0),
                                            compute_op=ALU.add).then_inc(row_landed[t % GT], 16)

            for r in range(ROUNDS):
                pool.wait_ge(staged_written, WRITES * GROUPS * (r + 1))
                if r == 1:
                    pool.wait_ge(x1_kept, GROUPS)
                with pool.Fori(0, TURNS) as i:
                    gather_edges(r, i)
                join_partitions(r)
                add_maxima(r)

        @block.scalar
        def _(act):
            act.sem_inc(turned_out, GT)
            act.sem_inc(product_out, GT)

            def stage(r, g):
                for k, end in tile_pairs:
                    act.wait_ge(product, r * TILES + g * GT + end + GT)
                    if k == 0 and not (r == 0 and isinstance(g, int)):
                        act.wait_ge(staged_written, WRITES * (r * GROUPS + g))
                    nc.scalar.copy(hist[:, GT + k:GT + end, :].rearrange("p k f -> p (k f)"),
                                   edge_ps[:, k // 2, 0:(end - k) * D]).then_inc(product_out, end - k)

            def feed_edges(r, i):
                for c in range(NCH):
                    act.wait_ge(pair_summed, (r * TURNS + i) * PAIRS + (c + 1) * CH // 2)
                    if r > 0:
                        act.dma_start(he_sb[:, c, :], a["he"][:, bass.ds((i * NCH + c) * (CH // 2) * P, CH // 2 * P)]
                                      ).then_inc(he_loaded[c], 16)
                    if c % 2 == 1:
                        j = (c - 1) * CH
                        nc.scalar.copy(idx_ring[:, j:j + 2 * CH], src_sb[:, bass.ds(i * BODY + j, 2 * CH)]
                                       ).then_inc(idx_ready, 1)
                if r < 2:
                    act.wait_ge(back_product, r * TILES + i + 1)
                    act.dma_start(back_T[:, :], (a["xT"] if r == 0 else x1T)[:, bass.ds(i * D, D)]).then_inc(back_loaded, 16)

            def copy_tile(r, g, k):
                act.wait_ge(row_landed[k], 16 * (r * GROUPS + g + 1))
                nc.scalar.copy(work[k], of_tile(hv_sb, g, k)).then_inc(tile_made, 1)

            def turn_out(r, g, copy_next=False):
                for k, end in tile_pairs:
                    act.wait_ge(tile_turned, r * TILES + g * GT + end)
                    act.wait_ge(product, (r + 1) * TILES + g * GT + end)
                    if r == 0 and k == 0:
                        act.wait_ge(x1T_written, 16 * (g + 1))
                    nc.scalar.copy(hist[:, k:end, :].rearrange("p k f -> p (k f)"),
                                   side_ps[:, k // 2, 0:(end - k) * D]).then_inc(turned_out, end - k)
                    if copy_next:
                        for t in range(k, end):
                            copy_tile(r, g + 1, t)

            def keep_normed(g):
                act.wait_ge(normed, (g + 1) * GT)
                nc.scalar.copy(of_group(x_sb, g).rearrange("p k f -> p (k f)"),
                               gath[:, GT:2 * GT, :].rearrange("p k f -> p (k f)")).then_inc(x1_kept, 1)

            def deviations(n, g):
                act.wait_ge(norm_step, NORM_STEPS * (n * GROUPS + g) + 3 * GT)
                nc.scalar.activation(std[:, :], mv[:, :, 1:2].rearrange("p k o -> p (k o)"), ACT.Sqrt,
                                     bias=eps_col[:, 0:1]).then_inc(std_ready, 1)

            stage(0, 0)
            with act.Fori(1, GROUPS) as g:
                stage(0, g)
            act.wait_ge(w_loaded, 16 * len(weight_loads))
            with act.Fori(0, TURNS) as i:
                feed_edges(0, i)
            deviations(0, 0)
            turn_out(0, 0)
            keep_normed(0)
            with act.Fori(1, GROUPS) as g:
                deviations(0, g)
                stage(1, g - 1)
                turn_out(0, g)
                keep_normed(g)
            stage(1, GROUPS - 1)
            act.wait_ge(x1T_written, 16 * (GROUPS + 1))
            with act.Fori(0, TURNS) as i:
                feed_edges(1, i)
            for k in range(GT):
                copy_tile(1, 0, k)
            with act.Fori(0, GROUPS - 1) as g:
                turn_out(1, g, copy_next=True)
            turn_out(1, GROUPS - 1)
            with act.Fori(0, TURNS) as i:
                feed_edges(2, i)
            for k in range(GT):
                copy_tile(2, 0, k)
            turn_out(2, 0, copy_next=True)
            with act.Fori(0, GROUPS - 2) as g:
                turn_out(2, g + 1, copy_next=True)
                deviations(1, g)
            turn_out(2, GROUPS - 1)
            deviations(1, GROUPS - 2)
            deviations(1, GROUPS - 1)

        @block.tensor
        def _(pe):
            T = nc.tensor
            pe.sem_inc(pair_summed, PAIRS)
            pe.sem_inc(product, GT)
            pe.sem_inc(back_product, 1)

            def linear(to, left, right, bias=None):
                for h in range(KH):
                    last = T.matmul(to, left[:, h * P:(h + 1) * P], right[:, h, :], start=(h == 0),
                                    stop=(bias is None and h == KH - 1))
                if bias is not None:
                    last = T.matmul(to, ones_bf[:, :], b_parts[:, bias, :], start=False, stop=True)
                return last

            def pick(q):
                pe.wait_ge(query, QSTEPS * q + 3)
                for lo, hi in ((0, 2 * D), (2 * D, STEPS + 1)):
                    last = T.matmul(query_ps[:, lo:hi], onehot[:, :], dst_f[:, lo:hi], start=True, stop=True)
                last.then_inc(dst_rows, 1)

            def first_tables(g):
                for k in range(GT):
                    pe.wait_ge(xT_landed[k // 2], 16 * g + 16)
                    pe.wait_ge(product_out, g * GT + pair_end[k])
                    linear(product_ps[k], xT_ring[k], w_diff).then_inc(product, 1)

            pe.wait_ge(setup_step, setup_at["conv weights"])
            with pe.Fori(0, GROUPS) as g:
                first_tables(g)

            pick(0)
            pe.wait_ge(setup_step, setup_at["b_in columns"])
            for m in range(KH):
                for h in range(KH):
                    T.matmul(side_ps[:, 2 + m, 0:D], w_inT[:, h, m * P:(m + 1) * P], w_n0[:, h, :], start=(h == 0),
                             stop=(h == KH - 1))
            for h in range(KH):
                last = T.matmul(side_ps[:, 2, D:], b_in_cols[:, h, :], w_n0[:, h, :], start=(h == 0), stop=(h == KH - 1))
            last.then_inc(weights_mult, 1)

            def messages(r, i):
                for c in range(NCH):
                    if r > 0:
                        pe.wait_ge(he_loaded[c], 16 * ((r - 1) * TURNS + i + 1))
                    for q in range(c * CH // 2, (c + 1) * CH // 2):
                        pe.wait_ge(state_done, ((r * TURNS + i) * PAIRS + q + 1) * 2)
                        bank = edge_ps[:, q % BANKS, :]
                        if r > 0:
                            at = (q % (CH // 2)) * P
                            T.matmul(bank, he_sb[:, c, at:at + P], w_e[r - 1][:, :], start=True, stop=False)
                        pe.wait_ge(gathered[q], 2 * 16 * (r * TURNS + i + 1))
                        T.matmul(bank, ident[:, :], gath[:, 2 * q:2 * q + 2, :].rearrange("p s f -> p (s f)"),
                                 start=(r == 0), stop=True).then_inc(pair_summed, 1)
                    if c == 1 and r < 2:
                        if r == 0:
                            pe.wait_ge(setup_step, setup_at["all"])
                        pe.wait_ge(back_loaded, 16 * (r * TILES + i + 1))
                        pe.wait_ge(back_kept, r * TILES + i + 1)
                        linear(back_ps, back_T, w_theta if r == 0 else w_in,
                               CONV if r == 0 else IN).then_inc(back_product, 1)
                if r == 0:
                    pick(i + 1)

            def turn(r, g, tiles=range(GT)):
                for k in tiles:
                    if r == 0:
                        pe.wait_ge(normed, g * GT + k + 1)
                    else:
                        pe.wait_ge(tile_made, (r - 1) * TILES + g * GT + k + 1)
                    pe.wait_ge(turned_out, r * TILES + g * GT + pair_end[k])
                    tile = (normal if r == 0 else work)[k]
                    for h in range(KH):
                        last = T.transpose(turned_ps[k][:, h * P:(h + 1) * P], tile[:, h * P:(h + 1) * P], ident[:, :])
                    last.then_inc(tile_turned, 1)

            def multiply(r, g, tiles=range(GT)):
                for k in tiles:
                    pe.wait_ge(turned_out, r * TILES + g * GT + k + 1 + GT)
                    if r < 2:
                        pe.wait_ge(product_out, (r + 1) * TILES + g * GT + pair_end[k])
                    else:
                        pe.wait_ge(norm_step, NORM_STEPS * (GROUPS + g - 1) + 2 * pair_end[k] - 2)
                    linear(product_ps[k], turned[k], (w_in_n0, w_n1, w_ro)[r],
                           (NEXT0, None, OUT)[r]).then_inc(product, 1)

            for r in range(ROUNDS):
                pe.wait_ge(product_out, (r + 1) * TILES + GT)
                with pe.Fori(0, TURNS) as i:
                    messages(r, i)
                pe.wait_ge(state_done, (r + 1) * STEPS + 2 * BANKS)
                if r == 0:
                    pe.wait_ge(query, QSTEPS * (TILES + 1) + 1)
                for h in range(KH):
                    last = T.transpose(side_ps[:, 0, h * P:(h + 1) * P], hist[:, BODY - 1, h * P:(h + 1) * P], ident[:, :])
                last.then_inc(fix_turned, 1)
                pe.wait_ge(fix_scanned, KH * (r + 1))
                for h in range(KH):
                    last = T.transpose(side_ps[:, 1, h * P:(h + 1) * P], fix_T[:, h, :], ident[:, :])
                last.then_inc(fix_back, 1)
                pe.wait_ge(fix_joined, r + 1)
                if r < 2:
                    with pe.Fori(0, GROUPS) as g:
                        turn(r, g)
                        multiply(r, g)
                else:
                    turn(2, 0)
                    with pe.Fori(0, GROUPS - 1) as g:
                        for k, end in tile_pairs:
                            turn(2, g + 1, range(k, end))
                            multiply(2, g, range(k, end))
                    multiply(2, GROUPS - 1)

def kernel(x, src, dst, edge_attr_64, L0_gnn_theta_w, L0_gnn_theta_b, L0_gnn_phi_w, L0_gnn_phi_b, L1_gnn_W_in,
           L1_gnn_b_in, L1_gnn_W_u0, L1_gnn_b_u0, L1_gnn_W_u1, L1_gnn_b_u1, L1_gnn_W_ro, L1_gnn_b_ro):
    import numpy as np
    import concourse.bacc as bacc
    from concourse.bass_utils import run_bass_kernel_spmd

    def pad(v, n, fill=0):
        v = np.asarray(v)
        return np.concatenate([v, np.full((n - v.shape[0],) + v.shape[1:], fill, v.dtype)])

    x_pad = pad(x, NPAD)
    dst_pad = pad(dst, SLOTS, NPAD).reshape(P, STEPS)
    he = pad(edge_attr_64, SLOTS).reshape(P, STEPS // 2, 2, ED)
    arrays = {
        "x": x_pad,
        "xT": x_pad.reshape(TILES, P, KH, P).transpose(3, 0, 2, 1).reshape(P, TILES * D),
        "src": pad(src, SLOTS).reshape(P, STEPS),
        "dst": dst_pad,
        "dst_last": dst_pad[:, STEPS - 1],
        "he": he.transpose(2, 3, 1, 0).reshape(P, STEPS // 2 * P),
        "theta_wT": np.asarray(L0_gnn_theta_w).T, "theta_b": L0_gnn_theta_b,
        "phi_wT": np.asarray(L0_gnn_phi_w).T, "phi_b": L0_gnn_phi_b,
        "W_in": L1_gnn_W_in, "W_inT": np.asarray(L1_gnn_W_in).T, "b_in": L1_gnn_b_in,
        "W_u0": L1_gnn_W_u0, "b_u0": L1_gnn_b_u0, "W_u1": L1_gnn_W_u1, "b_u1": L1_gnn_b_u1,
        "W_ro": L1_gnn_W_ro, "b_ro": L1_gnn_b_ro,
    }
    nc = bacc.Bacc("TRN2", target_bir_lowering=False, num_devices=1)
    given, aps = {}, {}
    for name, v in arrays.items():
        v = np.ascontiguousarray(v)
        given[f"in_{name}"] = v
        aps[name] = nc.dram_tensor(f"in_{name}", v.shape, mybir.dt.from_np(v.dtype), kind="ExternalInput").ap()
    aps["out"] = nc.dram_tensor("out_nodes", [NODES, D], mybir.dt.float32, kind="ExternalOutput").ap()
    gnn_kernel(nc, aps)
    return run_bass_kernel_spmd(nc, [given], core_ids=[0]).results[0]["out_nodes"]
```
